# Optimizing a Trainium2 kernel written in Bass

```python
import numpy as np
import jax
import jax.numpy as jnp

def _softmax(x, axis=-1):
    return jax.nn.softmax(x, axis=axis)

def _gelu(x):
    return jax.nn.gelu(x, approximate=True)

def _silu(x):
    return jax.nn.silu(x)

def _sigmoid(x):
    return jax.nn.sigmoid(x)

def _layernorm(x, axis=-1, eps=1e-05):
    m = jnp.mean(x, axis=axis, keepdims=True)
    v = jnp.var(x, axis=axis, keepdims=True)
    return (x - m) / jnp.sqrt(v + eps)

def _scatter_add(tgt, idx, src, axis=0):
    return tgt.at[idx].add(src)

def _segment_sum(src, seg, n):
    return jax.ops.segment_sum(src, seg, n)
kernel_name = 'mk_macaron_d1_jaxref_r8_54efab'

def setup_inputs(seed: int=0):
    np.random.seed(seed)
    _w = jnp.asarray

    def _L0_attn_setup():
        import jax, jax.numpy as jnp
        import numpy as np
        B, S, D, H = (2, 256, 128, 16)
        HD = D // H

        def _rope_cos_sin(seq_len, head_dim, base=10000.0):
            i = jnp.arange(head_dim // 2, dtype=jnp.float32)
            theta = base ** (-2.0 * i / head_dim)
            m = jnp.arange(seq_len, dtype=jnp.float32)
            ang = jnp.outer(m, theta)
            return (jnp.cos(ang), jnp.sin(ang))

        def _apply_rope(x, cos, sin):
            xr = x[..., 0::2]
            xi = x[..., 1::2]
            c = cos[None, :, None, :]
            s = sin[None, :, None, :]
            out_r = xr * c - xi * s
            out_i = xr * s + xi * c
            return jnp.stack([out_r, out_i], axis=-1).reshape(x.shape)
        key = jax.random.key(seed)
        ks = jax.random.split(key, 7)
        sc = 1.0 / np.sqrt(D)
        return {'x': jax.random.normal(ks[0], (B, S, D), dtype=jnp.float32), 'wq_w': jax.random.normal(ks[1], (D, D), dtype=jnp.float32) * sc, 'wq_b': jax.random.normal(ks[2], (D,), dtype=jnp.float32) * 0.01, 'wk_w': jax.random.normal(ks[3], (D, D), dtype=jnp.float32) * sc, 'wk_b': jax.random.normal(ks[4], (D,), dtype=jnp.float32) * 0.01, 'wv_w': jax.random.normal(ks[5], (D, D), dtype=jnp.float32) * sc, 'wv_b': jax.random.normal(ks[6], (D,), dtype=jnp.float32) * 0.01}
    _L0_attn_in = _L0_attn_setup()

    def _L0_ffn_setup():
        import jax, jax.numpy as jnp
        import numpy as np
        key = jax.random.key(seed)
        k1, k2, k3, k4 = jax.random.split(key, 4)
        B, T, M = (4, 256, 128)
        E, F = (16, 512)
        x = jax.random.normal(k1, (B, T, M), dtype=jnp.float32) * 0.02
        Wg = jax.random.normal(k2, (M, E), dtype=jnp.float32) * 0.02
        w1 = jax.random.normal(k3, (E, M, F), dtype=jnp.float32) * 0.02
        w2 = jax.random.normal(k4, (E, F, M), dtype=jnp.float32) * 0.02
        return {'x': x, 'Wg': Wg, 'w1': w1, 'w2': w2}
    _L0_ffn_in = _L0_ffn_setup()
    _d = {'L0_attn_x': _L0_attn_in['x'], 'L0_attn_wq_w': _L0_attn_in['wq_w'], 'L0_attn_wq_b': _L0_attn_in['wq_b'], 'L0_attn_wk_w': _L0_attn_in['wk_w'], 'L0_attn_wk_b': _L0_attn_in['wk_b'], 'L0_attn_wv_w': _L0_attn_in['wv_w'], 'L0_attn_wv_b': _L0_attn_in['wv_b'], 'L0_ffn_Wg': _L0_ffn_in['Wg'], 'L0_ffn_w1': _L0_ffn_in['w1'], 'L0_ffn_w2': _L0_ffn_in['w2']}
    _x0 = _d['L0_attn_x']
    _d['L0_attn_x'] = jax.random.normal(jax.random.fold_in(jax.random.key(seed), 1), (8, 512, 128), dtype=_x0.dtype)
    del _x0
    return _d

def reference(L0_attn_x, L0_attn_wq_w, L0_attn_wq_b, L0_attn_wk_w, L0_attn_wk_b, L0_attn_wv_w, L0_attn_wv_b, L0_ffn_Wg, L0_ffn_w1, L0_ffn_w2):

    def _L0_attn_ref(x, wq_w, wq_b, wk_w, wk_b, wv_w, wv_b):
        import jax, jax.numpy as jnp
        import numpy as np
        B, S, D, H = (2, 256, 128, 16)
        HD = D // H

        def _rope_cos_sin(seq_len, head_dim, base=10000.0):
            i = jnp.arange(head_dim // 2, dtype=jnp.float32)
            theta = base ** (-2.0 * i / head_dim)
            m = jnp.arange(seq_len, dtype=jnp.float32)
            ang = jnp.outer(m, theta)
            return (jnp.cos(ang), jnp.sin(ang))

        def _apply_rope(x, cos, sin):
            xr = x[..., 0::2]
            xi = x[..., 1::2]
            c = cos[None, :, None, :]
            s = sin[None, :, None, :]
            out_r = xr * c - xi * s
            out_i = xr * s + xi * c
            return jnp.stack([out_r, out_i], axis=-1).reshape(x.shape)
        bs, seq_len, dim = x.shape
        xq = (x @ wq_w.T + wq_b).reshape(bs, seq_len, H, HD)
        xk = (x @ wk_w.T + wk_b).reshape(bs, seq_len, H, HD)
        xv = (x @ wv_w.T + wv_b).reshape(bs, seq_len, H, HD)
        cos, sin = _rope_cos_sin(seq_len, HD)
        xq = _apply_rope(xq, cos, sin)
        xk = _apply_rope(xk, cos, sin)
        q = xq.transpose(0, 2, 1, 3)
        k = xk.transpose(0, 2, 1, 3)
        v = xv.transpose(0, 2, 1, 3)
        scores = jnp.einsum('bhqd,bhkd->bhqk', q, k) / np.sqrt(HD)
        attn = jax.nn.softmax(scores.astype(jnp.float32), axis=-1)
        out = jnp.einsum('bhqk,bhkd->bhqd', attn, v)
        return out.transpose(0, 2, 1, 3).reshape(bs, seq_len, dim)

    def _L0_ffn_ref(x, Wg, w1, w2):
        import jax, jax.numpy as jnp
        import numpy as np
        d = x.shape[-1]
        xr = x.reshape(-1, d)
        S = xr.shape[0]
        E = Wg.shape[1]
        C = (S + E - 1) // E
        gate = jax.nn.softmax(xr @ Wg, axis=-1)
        idx = jnp.argmax(gate, axis=1)
        gates_s = jnp.take_along_axis(gate, idx[:, None], axis=1)[:, 0]
        onehot = jax.nn.one_hot(idx, E, dtype=jnp.int32)
        loc = jnp.sum((jnp.cumsum(onehot, axis=0) - 1) * onehot, axis=1)
        valid = loc < C
        loc_pad = jnp.minimum(loc, C)
        dispatched = jnp.zeros((E, C + 1, d), dtype=x.dtype).at[idx, loc_pad].set(xr)
        dispatched = dispatched[:, :C]
        h = jax.nn.relu(jnp.einsum('ecm,emf->ecf', dispatched, w1))
        expert_out = jnp.einsum('ecf,efm->ecm', h, w2)
        gathered = expert_out[idx, jnp.minimum(loc, C - 1)]
        combined = gathered * (gates_s * valid.astype(x.dtype))[:, None]
        return combined.reshape(x.shape)
    x = L0_attn_x
    x = x + 0.5 * _L0_ffn_ref(_layernorm(x, axis=-1), L0_ffn_Wg, L0_ffn_w1, L0_ffn_w2)
    x = x + _L0_attn_ref(_layernorm(x, axis=-1), L0_attn_wq_w, L0_attn_wq_b, L0_attn_wk_w, L0_attn_wk_b, L0_attn_wv_w, L0_attn_wv_b)
    x = x + 0.5 * _L0_ffn_ref(_layernorm(x, axis=-1), L0_ffn_Wg, L0_ffn_w1, L0_ffn_w2)
    return x

_drawn_inputs = setup_inputs


def setup_inputs(seed=0):
    import zlib

    import numpy as np

    out = dict(_drawn_inputs(seed))
    spreads = {}
    factors = {'L0_attn_wq_b': 8.0,
     'L0_attn_wk_b': 8.0,
     'L0_attn_wv_b': 5.327,
     'L0_ffn_Wg': 8.0,
     'L0_ffn_w1': 8.0,
     'L0_ffn_w2': 8.0}
    for name, (base, spread) in spreads.items():
        noise = np.random.default_rng([zlib.crc32(name.encode()), seed]).standard_normal(out[name].shape)
        drawn = base * np.exp(spread * noise) if base else spread * noise
        out[name] = jnp.asarray(drawn.astype(out[name].dtype))
    for name, factor in factors.items():
        out[name] = (out[name] * factor).astype(out[name].dtype)
    return out
```

```python
from contextlib import ExitStack, nullcontext

import concourse.bass as bass
from concourse import mybir

ALU = mybir.AluOpType
ACT = mybir.ActivationFunctionType
AX = mybir.AxisListType
F32 = mybir.dt.float32
BF16 = mybir.dt.bfloat16
I32 = mybir.dt.int32
U32 = mybir.dt.uint32

P = 128
BATCH, SEQ, D = 8, 512, 128
TOKENS = BATCH * SEQ
TT = SEQ // P
EXPERTS, HID = 16, 512
CAP = TOKENS // EXPERTS
ST = CAP // P
FC = HID // P
ROW = D + 2
EPS = 1e-5
NOWHERE = 1 << 20
UNROLL = 4


class Steps:

    def __init__(self, eng, sem, start=0):
        self.eng, self.sem, self.start, self.n = eng, sem, start, 0

    def did(self, instruction):
        instruction.then_inc(self.sem, 1)
        self.n += 1

    def settle(self):
        self.eng.wait_ge(self.sem, self.start + self.n)
ROUTE_STEPS = 16
CONSTS = 12
HEADS, HEAD_DIM = 16, 8
QUADS = HEADS // 4
Q_PARTS = (0, 0, 1, 0, 1, 2)
K_PARTS = (0, 1, 0, 2, 1, 0)
SLOTS = len(Q_PARTS)
ROWS = SLOTS * HEAD_DIM
SHIFT_DMAS = 2 * 3


def macaron_block_kernel(nc, x, wq_t, wk_t, wv_t, qk_bias, v_bias, wg, w1, w2, rope, identity, count_mats,
                         expert_iota, token_number, out):
    SCALE = 1.0 / float(HEAD_DIM) ** 0.5

    with ExitStack() as ctx:
        def sb(name, shape, dt):
            return ctx.enter_context(nc.sbuf_tensor(name, shape, dt))

        def sem(name):
            return ctx.enter_context(nc.semaphore(name))

        x1 = nc.dram_tensor("x1", (TOKENS, D), F32).ap()
        slots = [nc.dram_tensor(f"slots{k}", (TOKENS, ROW), F32).ap() for k in range(2)]
        rows_of = [x1, out]

        ident = sb("ident", [P, P], F32)
        counters = sb("counters", [P, 2, P], BF16)
        iota_e = sb("iota_e", [P, EXPERTS], F32)
        iota_low = sb("iota_low", [P, EXPERTS], F32)
        numbers = sb("numbers", [P, TOKENS // P], I32)
        wg_sb = sb("wg_sb", [P, EXPERTS], F32)
        w2_sb = sb("w2_sb", [P, EXPERTS, FC, D], F32)
        w1_ring = sb("w1_ring", [P, UNROLL, HID], F32)
        empty = sb("empty", [P, ROW], F32)

        stage = sb("stage", [P, 2, TT, ROW], F32)
        xn = sb("xn", [P, 2, TT, D], F32)
        xn_t = sb("xn_t", [P, 2, SEQ], F32)
        stats = sb("stats", [P, TT, 6], F32)
        moments = sb("moments", [P, TT, 2], F32)
        minus_half = sb("minus_half", [P, TT], F32)
        spread = sb("spread", [P, TT], F32)
        rstd = sb("rstd", [P, TT], F32)
        top = sb("top", [P, TT], F32)
        below = sb("below", [P, TT, EXPERTS], F32)
        tied = sb("tied", [P, TT, EXPERTS], F32)
        first = sb("first", [P, TT], F32)
        onehot = sb("onehot", [P, TT, EXPERTS], BF16)
        gate_exp = sb("gate_exp", [P, TT, EXPERTS], F32)
        place = sb("place", [P, TT, EXPERTS], F32)
        carry = sb("carry", [P, EXPERTS], F32)
        loc = sb("loc", [P, TT], F32)
        base = sb("base", [P, TT], F32)
        over = sb("over", [P, TT], F32)
        half = sb("half", [P, TT], F32)
        gate_sum = sb("gate_sum", [P, TT], F32)
        dest = sb("dest", [P, 2, TT], I32)

        slot_rows = sb("slot_rows", [P, UNROLL, ST, ROW], F32)
        new_rows = sb("new_rows", [P, UNROLL, ST, ROW], F32)
        slot_stats = sb("slot_stats", [P, ST, 6], F32)
        slot_moments = sb("slot_moments", [P, 2, ST, 2], F32)
        slot_spread = sb("slot_spread", [P, 2, ST], F32)
        slot_rstd = sb("slot_rstd", [P, 2, ST], F32)
        slot_xn = sb("slot_xn", [P, 2, ST, D], F32)
        slot_xn_t = sb("slot_xn_t", [P, 2, CAP], F32)
        hidden = sb("hidden", [P, 2, FC, CAP], F32)

        psum = ctx.enter_context(nc.psum_tensor("psum", [P, 8, 512], F32))

        consts_loaded = sem("consts_loaded")
        w2_loaded = sem("w2_loaded")
        x_passed = sem("x_passed")
        x_loaded = [sem(f"x_loaded{s}") for s in range(2)]
        empty_ready = sem("empty_ready")
        waits_passed = sem("waits_passed")
        slots_cleared = sem("slots_cleared")
        w1_loaded = [sem(f"w1_loaded{k}") for k in range(UNROLL)]
        w1_used = sem("w1_used")
        slots_loaded = [sem(f"slots_loaded{k}") for k in range(UNROLL)]
        rows_written = [sem(f"rows_written{k}") for k in range(UNROLL)]
        dispatched = [sem(f"dispatched{s}") for s in range(2)]
        xn_ready = sem("xn_ready")
        xn_t_placed = sem("xn_t_placed")
        xn_t_ready = sem("xn_t_ready")
        logits_ready = sem("logits_ready")
        below_ready = sem("below_ready")
        gate_exp_ready = sem("gate_exp_ready")
        onehot_ready = sem("onehot_ready")
        place_ready = sem("place_ready")
        route_ready = sem("route_ready")
        route_step = sem("route_step")
        moments_ready = sem("moments_ready")
        rstd_ready = sem("rstd_ready")
        slot_stats_ready = sem("slot_stats_ready")
        slot_moments_ready = sem("slot_moments_ready")
        slot_rstd_ready = sem("slot_rstd_ready")
        slot_xn_ready = sem("slot_xn_ready")
        slot_xn_t_placed = sem("slot_xn_t_placed")
        slot_xn_t_ready = sem("slot_xn_t_ready")
        hidden_placed = sem("hidden_placed")
        hidden_ready = sem("hidden_ready")
        y_placed = sem("y_placed")
        y_used = sem("y_used")

        wq_sb = sb("wq_sb", [P, 2, D], F32)
        wk_sb = sb("wk_sb", [P, 2, D], F32)
        wv_sb = sb("wv_sb", [P, D], F32)
        bias_sb = sb("bias_sb", [P, 4], F32)
        v_bias_sb = sb("v_bias_sb", [P, D], F32)
        rope_sb = sb("rope_sb", [P, 2, SEQ], F32)
        prep_x = sb("prep_x", [P, TT, D], F32)
        prep_stats = sb("prep_stats", [P, TT, 6], F32)
        prep_moments = sb("prep_moments", [P, TT, 2], F32)
        prep_spread = sb("prep_spread", [P, TT], F32)
        prep_rstd = sb("prep_rstd", [P, TT], F32)
        prep_xn = sb("prep_xn", [P, TT, D], F32)
        prep_xn_t = sb("prep_xn_t", [P, SEQ], F32)
        proj = sb("proj", [P, 4, SEQ], F32)
        turned = sb("turned", [P, 2, SEQ], F32)
        parts = sb("parts", [P, 2, 3, SEQ], BF16)
        v_flat = sb("v_flat", [P, BATCH, TT, D], F32)
        v_ring = sb("v_ring", [P, QUADS, TT, 4, 32], F32)
        q_ring = sb("q_ring", [P, QUADS, 2, SEQ], BF16)
        k_ring = sb("k_ring", [P, QUADS, 2, SEQ], BF16)
        neg_max = sb("neg_max", [P, 2, 16], F32)
        shift = sb("shift", [16, P], F32)
        shift_rest = sb("shift_rest", [16, P], F32)
        shift_parts = sb("shift_parts", [16, 3, P], BF16)
        probs = sb("probs", [P, TT, 4, SEQ], F32)
        out_t = sb("out_t", [P, SEQ], F32)
        weight = sb("weight", [P, TT, 4], F32)
        attended = sb("attended", [P, TT, D], F32)
        residual = sb("residual", [P, TT, D], F32)
        qk_rows = nc.dram_tensor("qk_rows", (BATCH, 2, 2 * QUADS, SLOTS, 16, SEQ), BF16).ap()

        prep_x_loaded = sem("prep_x_loaded")
        prep_stats_ready = sem("prep_stats_ready")
        prep_moments_ready = sem("prep_moments_ready")
        prep_rstd_ready = sem("prep_rstd_ready")
        prep_xn_ready = sem("prep_xn_ready")
        prep_xn_t_placed = sem("prep_xn_t_placed")
        prep_xn_t_ready = sem("prep_xn_t_ready")
        proj_placed = sem("proj_placed")
        proj_kept = sem("proj_kept")
        v_placed = sem("v_placed")
        v_kept = sem("v_kept")
        v_filled = sem("v_filled")
        ring_cleared = sem("ring_cleared")
        rope_step = sem("rope_step")
        roped = sem("roped")
        first_part_ready = sem("first_part_ready")
        rest_ready = sem("rest_ready")
        second_part_ready = sem("second_part_ready")
        parts_ready = sem("parts_ready")
        parts_written = [sem(f"parts_written{c}") for c in range(2)]
        quad_loaded = [sem(f"quad_loaded{g}") for g in range(QUADS)]
        shift_loaded = sem("shift_loaded")
        max_placed = sem("max_placed")
        max_used = sem("max_used")
        shift_placed = sem("shift_placed")
        shift_kept = sem("shift_kept")
        shift_first = sem("shift_first")
        shift_step = sem("shift_step")
        shift_ready = sem("shift_ready")
        score_placed = sem("score_placed")
        exp_done = sem("exp_done")
        o_placed = sem("o_placed")
        o_kept = sem("o_kept")
        o_turned = sem("o_turned")
        weight_ready = sem("weight_ready")
        attended_ready = sem("attended_ready")
        residual_loaded = sem("residual_loaded")
        x2_ready = sem("x2_ready")
        x2_passed = sem("x2_passed")

        block = ctx.enter_context(nc.Block())


        def pass_wait(eng):
            eng.sem_inc(waits_passed, 1)

        def measure(dve, steps, s):
            for t in range(TT):
                i = nc.vector.bn_stats(stats[:, t, :], stage[:, s, t, 0:D])
            steps.did(i)
            steps.settle()
            pass_wait(dve)
            for t in range(TT):
                i = nc.vector.bn_aggr(moments[:, t, :], stats[:, t, :])
            steps.did(i)
            steps.settle()
            nc.vector.tensor_scalar(spread[:, :], moments[:, :, 1], EPS, None, ALU.add).then_inc(moments_ready, 1)

        def invert_deviation(pool, r):
            pool.wait_ge(moments_ready, r + 1)
            nc.gpsimd.tensor_tensor(rstd[:, :], spread[:, :], minus_half[:, :], ALU.pow).then_inc(rstd_ready, 1)

        def normalize(dve, r, s):
            dve.wait_ge(rstd_ready, r + 1)
            for t in range(TT):
                i = nc.vector.tensor_scalar(xn[:, s, t, :], stage[:, s, t, 0:D], moments[:, t, 0:1],
                                            rstd[:, t:t + 1], ALU.subtract, ALU.mult)
            i.then_inc(xn_ready, 1)

        def choose(dve, steps, r, bank):
            logits = psum[:, bank, 0:TT * EXPERTS].rearrange("p (t e) -> p t e", e=EXPERTS)
            dve.wait_ge(logits_ready, r + 1)
            steps.did(nc.vector.tensor_reduce(top[:, :], logits, AX.X, ALU.max))
            steps.settle()
            nc.vector.tensor_tensor(below[:, :, :], logits, top[:, :].unsqueeze(2).broadcast_to([P, TT, EXPERTS]),
                                    ALU.subtract).then_inc(below_ready, 1)
            dve.wait_ge(below_ready, r + 1)
            steps.did(nc.vector.tensor_scalar(tied[:, :, :], below[:, :, :], 0.0, -float(EXPERTS),
                                              ALU.is_ge, ALU.mult))
            steps.settle()
            steps.did(nc.vector.tensor_tensor(tied[:, :, :], tied[:, :, :],
                                              iota_e[:, :].unsqueeze(1).broadcast_to([P, TT, EXPERTS]), ALU.add))
            steps.settle()
            steps.did(nc.vector.tensor_reduce(first[:, :], tied[:, :, :], AX.X, ALU.min))
            steps.settle()
            nc.vector.tensor_tensor(onehot[:, :, :], iota_low[:, :].unsqueeze(1).broadcast_to([P, TT, EXPERTS]),
                                    first[:, :].unsqueeze(2).broadcast_to([P, TT, EXPERTS]),
                                    ALU.is_equal).then_inc(onehot_ready, 1)
            steps.did(nc.vector.tensor_scalar(base[:, :], first[:, :], float(EXPERTS), float(CAP),
                                              ALU.add, ALU.mult))

        def route(dve, steps, r, s, bank, b):
            earlier = psum[:, bank, 64:64 + TT * EXPERTS].rearrange("p (t e) -> p t e", e=EXPERTS)
            total = psum[:, bank, 128:128 + EXPERTS]
            dve.wait_ge(place_ready, r + 1)
            dve.wait_ge(onehot_ready, r + 1)
            steps.did(nc.vector.tensor_tensor(place[:, :, :], earlier,
                                              carry[:, :].unsqueeze(1).broadcast_to([P, TT, EXPERTS]), ALU.add))
            steps.settle()
            steps.did(nc.vector.tensor_tensor(place[:, :, :], place[:, :, :], onehot[:, :, :], ALU.mult))
            steps.did(nc.vector.tensor_tensor(carry[:, :], total, carry[:, :], ALU.add))
            steps.settle()
            steps.did(nc.vector.tensor_reduce(loc[:, :], place[:, :, :], AX.X, ALU.add))
            dve.wait_ge(gate_exp_ready, r + 1)
            steps.did(nc.vector.tensor_reduce(gate_sum[:, :], gate_exp[:, :, :], AX.X, ALU.add))
            steps.settle()
            steps.did(nc.vector.tensor_tensor(base[:, :], base[:, :], loc[:, :], ALU.add))
            steps.did(nc.vector.tensor_scalar(over[:, :], loc[:, :], float(CAP), float(NOWHERE), ALU.is_ge, ALU.mult))
            steps.did(nc.vector.tensor_scalar(half[:, :], loc[:, :], float(CAP), 0.5, ALU.is_lt, ALU.mult))
            steps.did(nc.vector.reciprocal(gate_sum[:, :], gate_sum[:, :]))
            steps.settle()
            nc.vector.tensor_tensor(dest[:, s, :], base[:, :], over[:, :], ALU.add)
            nc.vector.tensor_tensor(stage[:, s, :, D + 1], half[:, :], gate_sum[:, :], ALU.mult)
            nc.vector.tensor_copy(stage[:, s, :, D].bitcast(I32),
                                  numbers[:, bass.ds(b * TT, TT)]).then_inc(route_ready, 1)

        def turn_tokens(pe, r, s, bank):
            pe.wait_ge(xn_ready, r + 1)
            for t in range(TT):
                i = nc.tensor.transpose(psum[:, bank, t * P:(t + 1) * P], xn[:, s, t, :], ident[:, :])
            i.then_inc(xn_t_placed, 1)

        def gate_logits(pe, r, s, bank):
            pe.wait_ge(xn_t_ready, r + 1)
            for t in range(TT):
                i = nc.tensor.matmul(psum[:, bank, t * EXPERTS:(t + 1) * EXPERTS], xn_t[:, s, t * P:(t + 1) * P],
                                     wg_sb[:, :], start=True, stop=True)
            i.then_inc(logits_ready, 1)

        def count_places(pe, r, bank):
            pe.wait_ge(onehot_ready, r + 1)
            flat = onehot[:, :, :].rearrange("p t e -> p (t e)")
            nc.tensor.matmul(psum[:, bank, 64:64 + TT * EXPERTS], counters[:, 0, :], flat, start=True, stop=False,
                             skip_group_check=True)
            for t in range(TT - 1):
                nc.tensor.matmul(psum[:, bank, 64 + (t + 1) * EXPERTS:64 + TT * EXPERTS], counters[:, 1, :],
                                 onehot[:, t, :].unsqueeze(1).broadcast_to([P, TT - 1 - t, EXPERTS]),
                                 start=False, stop=t == TT - 2, skip_group_check=True)
            for t in range(TT):
                i = nc.tensor.matmul(psum[:, bank, 128:128 + EXPERTS], counters[:, 1, :], onehot[:, t, :],
                                     start=False, stop=t == TT - 1, skip_group_check=True)
            i.then_inc(place_ready, 1)

        def keep_turned(act, r, s, bank):
            act.wait_ge(xn_t_placed, r + 1)
            nc.scalar.copy(xn_t[:, s, :], psum[:, bank, :]).then_inc(xn_t_ready, 1)

        def gate_exponentials(act, r):
            act.wait_ge(below_ready, r + 1)
            nc.scalar.activation(gate_exp[:, :, :], below[:, :, :], ACT.Exp).then_inc(gate_exp_ready, 1)

        def scatter_tokens(pool, r, s, layer):
            pool.wait_ge(route_ready, r + 1)
            pass_wait(pool)
            for t in range(TT):
                pool.indirect_dma_start(
                    out=slots[layer][:, :],
                    out_offset=bass.IndirectOffsetOnAxis(ap=dest[:, s, t:t + 1].bitcast(U32), axis=0),
                    in_=stage[:, s, t, :], in_offset=None, bounds_check=TOKENS - 1,
                    oob_is_err=False).then_inc(dispatched[s], 16)


        def load_w1(sp, layer, i, k):
            sp.wait_ge(w1_used, i * UNROLL + (layer * EXPERTS + k + 1))
            sp.dma_start(w1_ring[:, k, :], w1[i * UNROLL + k]).then_inc(w1_loaded[k], 16)

        def load_slots(sp, layer, i, k):
            sp.wait_ge(y_used, i * UNROLL + (layer * EXPERTS + k + 1))
            sp.dma_start(slot_rows[:, k, :, :],
                         slots[layer][bass.ds((i * UNROLL + k) * CAP, CAP), :].rearrange("(s p) c -> p s c", p=P)
                         ).then_inc(slots_loaded[k], 16)

        def load_experts(sp, layer):
            for s in range(2):
                sp.wait_ge(dispatched[s], all_dispatched(s, layer))
            for k in range(UNROLL):
                load_slots(sp, layer, 0, k)
            with sp.Fori(0, EXPERTS // UNROLL - 1) as i:
                for k in range(UNROLL):
                    load_w1(sp, layer, i + 1, k)
                    load_slots(sp, layer, i + 1, k)

        def all_dispatched(s, layer):
            return 16 * TT * BATCH // 2 * (1 + 2 * layer * (s == 0))

        def measure_slots(dve, n, turn, k):
            dve.wait_ge(slots_loaded[k], (turn + 1) * 16)
            for s in range(ST):
                i = nc.vector.bn_stats(slot_stats[:, s, :], slot_rows[:, k, s, 0:D])
            i.then_inc(slot_stats_ready, 1)
            dve.wait_ge(slot_stats_ready, 2 * n + 1)
            pass_wait(dve)
            for s in range(ST):
                i = nc.vector.bn_aggr(slot_moments[:, k % 2, s, :], slot_stats[:, s, :])
            i.then_inc(slot_stats_ready, 1)
            dve.wait_ge(slot_stats_ready, 2 * n + 2)
            nc.vector.tensor_scalar(slot_spread[:, k % 2, :], slot_moments[:, k % 2, :, 1], EPS, None, ALU.add
                                    ).then_inc(slot_moments_ready, 1)

        def invert_slot_deviation(pool, n, k):
            pool.wait_ge(slot_moments_ready, n + 1)
            nc.gpsimd.tensor_tensor(slot_rstd[:, k % 2, :], slot_spread[:, k % 2, :], minus_half[:, 0:ST], ALU.pow
                                    ).then_inc(slot_rstd_ready, 1)

        def normalize_slots(dve, n, k):
            dve.wait_ge(slot_rstd_ready, n + 1)
            for s in range(ST):
                i = nc.vector.tensor_scalar(slot_xn[:, k % 2, s, :], slot_rows[:, k, s, 0:D],
                                            slot_moments[:, k % 2, s, 0:1], slot_rstd[:, k % 2, s:s + 1],
                                            ALU.subtract, ALU.mult)
            i.then_inc(slot_xn_ready, 1)

        def add_expert(dve, n, turn, k):
            dve.wait_ge(y_placed, n + 1)
            dve.wait_ge(rows_written[k], turn * (16 * ST))
            nc.vector.tensor_copy(new_rows[:, k, :, D].bitcast(I32), slot_rows[:, k, :, D].bitcast(I32))
            for s in range(ST):
                i = nc.vector.scalar_tensor_tensor(new_rows[:, k, s, 0:D], psum[:, 6 + k % 2, s * D:(s + 1) * D],
                                                   slot_rows[:, k, s, D + 1:D + 2], slot_rows[:, k, s, 0:D],
                                                   ALU.mult, ALU.add)
            i.then_inc(y_used, 1)

        def turn_slots(pe, n, k):
            pe.wait_ge(slot_xn_ready, n + 1)
            for s in range(ST):
                i = nc.tensor.transpose(psum[:, k % 2, s * P:(s + 1) * P], slot_xn[:, k % 2, s, :], ident[:, :])
            i.then_inc(slot_xn_t_placed, 1)

        def expert_in(pe, n, turn, k):
            pe.wait_ge(slot_xn_t_ready, n + 1)
            pe.wait_ge(w1_loaded[k], (turn + 1) * 16)
            for c in range(FC):
                i = nc.tensor.matmul(psum[:, 2 + 2 * (k % 2) + c // 2, (c % 2) * CAP:(c % 2 + 1) * CAP],
                                     w1_ring[:, k, c * P:(c + 1) * P], slot_xn_t[:, k % 2, :],
                                     start=True, stop=True)
                if c % 2 == 1:
                    i.then_inc(hidden_placed, 1)

        def expert_out(pe, n, e, k):
            pe.wait_ge(hidden_ready, 2 * n + 2)
            pe.wait_ge(y_used, n + (UNROLL - 1))
            for s in range(ST):
                for c in range(FC):
                    i = nc.tensor.matmul(psum[:, 6 + k % 2, s * D:(s + 1) * D], hidden[:, k % 2, c, s * P:(s + 1) * P],
                                         w2_sb[:, e, c, :], start=c == 0, stop=c == FC - 1)
                    if s == 0 and c == 0:
                        i.then_inc(w1_used, 1)
            i.then_inc(y_placed, 1)

        def keep_slots_turned(act, n, k):
            act.wait_ge(slot_xn_t_placed, n + 1)
            nc.scalar.copy(slot_xn_t[:, k % 2, :], psum[:, k % 2, 0:CAP]).then_inc(slot_xn_t_ready, 1)

        def rectify(act, n, k):
            for c in range(0, FC, 2):
                act.wait_ge(hidden_placed, 2 * n + c // 2 + 1)
                nc.scalar.activation(hidden[:, k % 2, c:c + 2, :],
                                     psum[:, 2 + 2 * (k % 2) + c // 2, :].rearrange("p (c n) -> p c n", c=2),
                                     ACT.Relu).then_inc(hidden_ready, 1)

        def scatter_rows(pool, n, k, layer):
            pool.wait_ge(y_used, n + (UNROLL + 1))
            pass_wait(pool)
            for s in range(ST):
                pool.indirect_dma_start(
                    out=rows_of[layer][:, :],
                    out_offset=bass.IndirectOffsetOnAxis(ap=new_rows[:, k, s, D:D + 1].bitcast(U32), axis=0),
                    in_=new_rows[:, k, s, 0:D], in_offset=None, bounds_check=TOKENS - 1,
                    oob_is_err=False).then_inc(rows_written[k], 16)

        def pool_experts(pool, layer):
            def body(i, last):
                for k in range(UNROLL):
                    n = i * UNROLL + (layer * EXPERTS + k)
                    if not (last and k + 3 >= UNROLL):
                        invert_slot_deviation(pool, n + 3, (k + 3) % UNROLL)
                    scatter_rows(pool, n, k, layer)
            n = layer * EXPERTS
            for k in range(3):
                invert_slot_deviation(pool, n + k, k)
            with pool.Fori(0, EXPERTS // UNROLL - 1) as i:
                body(i, False)
            body(EXPERTS // UNROLL - 1, True)

        def pe_experts(pe, layer):
            def body(i, last):
                for k in range(UNROLL):
                    e = i * UNROLL + k
                    n = i * UNROLL + (layer * EXPERTS + k)
                    turn = i + layer * (EXPERTS // UNROLL)
                    if not (last and k + 1 >= UNROLL):
                        expert_in(pe, n + 1, turn + (k + 1) // UNROLL, (k + 1) % UNROLL)
                    if not (last and k + 2 >= UNROLL):
                        turn_slots(pe, n + 2, (k + 2) % UNROLL)
                    expert_out(pe, n, e, k)
            n = layer * EXPERTS
            turn_slots(pe, n, 0)
            turn_slots(pe, n + 1, 1)
            expert_in(pe, n, layer * (EXPERTS // UNROLL), 0)
            with pe.Fori(0, EXPERTS // UNROLL - 1) as i:
                body(i, False)
            body(EXPERTS // UNROLL - 1, True)

        def act_experts(act, layer):
            def body(i, last):
                for k in range(UNROLL):
                    n = i * UNROLL + (layer * EXPERTS + k)
                    if not (last and k + 1 >= UNROLL):
                        rectify(act, n + 1, (k + 1) % UNROLL)
                    if not (last and k + 2 >= UNROLL):
                        keep_slots_turned(act, n + 2, (k + 2) % UNROLL)
            n = layer * EXPERTS
            keep_slots_turned(act, n, 0)
            keep_slots_turned(act, n + 1, 1)
            rectify(act, n, 0)
            with act.Fori(0, EXPERTS // UNROLL - 1) as i:
                body(i, False)
            body(EXPERTS // UNROLL - 1, True)

        def dve_experts(dve, layer):
            def body(i, last):
                for k in range(UNROLL):
                    n = i * UNROLL + (layer * EXPERTS + k)
                    turn = i + layer * (EXPERTS // UNROLL)
                    if not (last and k + 2 >= UNROLL):
                        dve.wait_ge(slot_xn_t_placed, n + 1)
                        normalize_slots(dve, n + 2, (k + 2) % UNROLL)
                    if not (last and k + 3 >= UNROLL):
                        measure_slots(dve, n + 3, turn + (k + 3) // UNROLL, (k + 3) % UNROLL)
                    add_expert(dve, n, turn, k)
            n, turn = layer * EXPERTS, layer * (EXPERTS // UNROLL)
            for k in range(2):
                measure_slots(dve, n + k, turn, k)
            for k in range(2):
                normalize_slots(dve, n + k, k)
            measure_slots(dve, n + 2, turn, 2)
            with dve.Fori(0, EXPERTS // UNROLL - 1) as i:
                body(i, False)
            body(EXPERTS // UNROLL - 1, True)


        MISC, OUT_T = 1, 0
        SCORE, MAXIMA = 2, 4

        def load_prep(sp, n):
            sp.wait_ge(prep_xn_ready, n)
            sp.dma_start(prep_x[:, :, :], x1[bass.ds(n * SEQ, SEQ), :].rearrange("(t p) d -> p t d", p=P)
                         ).then_inc(prep_x_loaded, 16)

        def prep_measure(dve, n):
            dve.wait_ge(prep_x_loaded, (n + 1) * 16)
            for t in range(TT):
                i = nc.vector.bn_stats(prep_stats[:, t, :], prep_x[:, t, :])
            i.then_inc(prep_stats_ready, 1)
            dve.wait_ge(prep_stats_ready, n * 2 + 1)
            pass_wait(dve)
            for t in range(TT):
                i = nc.vector.bn_aggr(prep_moments[:, t, :], prep_stats[:, t, :])
            i.then_inc(prep_stats_ready, 1)
            dve.wait_ge(prep_stats_ready, n * 2 + 2)
            nc.vector.tensor_scalar(prep_spread[:, :], prep_moments[:, :, 1], EPS, None, ALU.add
                                    ).then_inc(prep_moments_ready, 1)

        def prep_normalize(pool, n):
            pool.wait_ge(prep_moments_ready, n + 1)
            nc.gpsimd.tensor_tensor(prep_rstd[:, :], prep_spread[:, :], minus_half[:, :], ALU.pow
                                    ).then_inc(prep_rstd_ready, 1)
            pool.wait_ge(prep_rstd_ready, n + 1)
            pool.wait_ge(prep_xn_t_placed, n)
            pass_wait(pool)
            for t in range(TT):
                i = nc.gpsimd.tensor_scalar(prep_xn[:, t, :], prep_x[:, t, :], prep_moments[:, t, 0:1],
                                            prep_rstd[:, t:t + 1], ALU.subtract, ALU.mult)
            i.then_inc(prep_xn_ready, 1)

        def prep_turn(pe, n):
            pe.wait_ge(prep_xn_ready, n + 1)
            for t in range(TT):
                i = nc.tensor.transpose(psum[:, MISC, t * P:(t + 1) * P], prep_xn[:, t, :], ident[:, :])
            i.then_inc(prep_xn_t_placed, 1)

        def prep_keep_turned(act, n):
            act.wait_ge(prep_xn_t_placed, n + 1)
            nc.scalar.copy(prep_xn_t[:, :], psum[:, MISC, :]).then_inc(prep_xn_t_ready, 1)

        def project(pe, n, c):
            pe.wait_ge(prep_xn_t_ready, n + 1)
            w = (wq_sb, wk_sb)[c // 2][:, c % 2, :]
            nc.tensor.matmul(psum[:, MISC, :], w, prep_xn_t[:, :], start=True, stop=True).then_inc(proj_placed, 1)

        def keep_projection(act, n, c):
            act.wait_ge(proj_placed, n * 4 + (c + 1))
            act.wait_ge(roped, n * 2 + (1 + c // 2))
            nc.scalar.activation(proj[:, c, :], psum[:, MISC, :], ACT.Identity, bias=bias_sb[:, c:c + 1]
                                 ).then_inc(proj_kept, 1)

        def project_v(pe, n):
            pe.wait_ge(prep_xn_t_ready, n + 1)
            for t in range(TT):
                i = nc.tensor.matmul(psum[:, MISC, t * D:(t + 1) * D], prep_xn_t[:, t * P:(t + 1) * P], wv_sb[:, :],
                                     start=True, stop=True)
            i.then_inc(v_placed, 1)

        def keep_v(act, n):
            act.wait_ge(v_placed, n + 1)
            nc.scalar.copy(v_flat[:, bass.ds(n, 1), :, :].squeeze(1),
                           psum[:, MISC, :].rearrange("p (t d) -> p t d", t=TT)).then_inc(v_kept, 1)

        def rotate(pool, n, c):
            pool.wait_ge(proj_kept, n * 4 + (2 * c + 2))
            nc.gpsimd.tensor_tensor(proj[:, 2 * c, :], proj[:, 2 * c, :], rope_sb[:, 0, :], ALU.mult)
            nc.gpsimd.tensor_tensor(proj[:, 2 * c + 1, :], proj[:, 2 * c + 1, :], rope_sb[:, 1, :], ALU.mult
                                    ).then_inc(rope_step, 1)
            pool.wait_ge(rope_step, n * 2 + (c + 1))
            nc.gpsimd.tensor_tensor(turned[:, c, :], proj[:, 2 * c, :], proj[:, 2 * c + 1, :], ALU.add
                                    ).then_inc(roped, 1)

        def keep_first_part(act, n, c):
            act.wait_ge(roped, n * 2 + (c + 3))
            act.wait_ge(parts_written[c], n * (16 * SLOTS))
            nc.scalar.copy(parts[:, c, 0, :], turned[:, c, :]).then_inc(first_part_ready, 1)

        def take_rest(pool, n, c):
            pool.wait_ge(first_part_ready, n * 2 + (c + 1))
            nc.gpsimd.tensor_tensor(turned[:, c, :], turned[:, c, :], parts[:, c, 0, :], ALU.subtract
                                    ).then_inc(rest_ready, 1)

        def keep_second_part(act, n, c):
            act.wait_ge(rest_ready, n * 2 + (c + 1))
            nc.scalar.copy(parts[:, c, 1, :], turned[:, c, :]).then_inc(second_part_ready, 1)

        def keep_third_part(pool, n, c):
            pool.wait_ge(second_part_ready, n * 2 + (c + 1))
            nc.gpsimd.tensor_tensor(parts[:, c, 2, :], turned[:, c, :], parts[:, c, 1, :], ALU.subtract
                                    ).then_inc(parts_ready, 1)

        def write_parts(sp, n, c):
            sp.wait_ge(parts_ready, n * 2 + (c + 1))
            for slot, part in enumerate((Q_PARTS, K_PARTS)[c]):
                sp.dma_start(qk_rows[bass.ds(n, 1), c, :, slot, :, :].squeeze(0), parts[:, c, part, :]).then_inc(parts_written[c], 16)

        def load_quad(sp, n, g):
            for c in range(2):
                sp.wait_ge(parts_written[c], (n + 1) * (16 * SLOTS))
            for c, ring in enumerate((q_ring, k_ring)):
                for h in range(2):
                    src = qk_rows[bass.ds(n, 1), c, 2 * g + h, :, :, :].squeeze(0)
                    sp.dma_start(ring[64 * h:64 * h + SLOTS * HEAD_DIM, g, :, :].rearrange("p h s -> p (h s)"),
                                 src.rearrange("s (d h) t -> (s d) (h t)", h=2)).then_inc(quad_loaded[g], 16)

        def fill_v(pool, n, g, q):
            pool.wait_ge(v_kept, n + 1)
            flat = v_flat[:, bass.ds(n, 1), :, :].squeeze(1)
            nc.gpsimd.tensor_tensor(
                v_ring[:, g, :, :, 0:HEAD_DIM],
                flat[:, :, 32 * g:32 * g + 32].rearrange("p t (h d) -> p t h d", h=4),
                v_bias_sb[:, 32 * g:32 * g + 32].rearrange("p (h d) -> p h d", h=4).unsqueeze(1)
                .broadcast_to([P, TT, 4, HEAD_DIM]), ALU.add).then_inc(v_filled, 1)

        def max_tile(pe, q, g, w):
            head, tile = divmod(w, TT)
            r, h = 64 * (head % 2), head // 2
            if w % 2 == 0:
                pe.wait_ge(max_used, q * 8 + (w // 2 + 1))
            i = nc.tensor.matmul(psum[:, MAXIMA + w % 4, :], q_ring[r:r + ROWS, g, h, tile * P:(tile + 1) * P],
                                 k_ring[r:r + ROWS, g, h, :], start=True, stop=True)
            if w % 2 == 1:
                i.then_inc(max_placed, 1)

        def take_max(dve, q, g, pair):
            head, half = divmod(pair, 2)
            col = (head % 2) * 8 + (head // 2) * 4 + half * 2
            bank = MAXIMA + 2 * (pair % 2)
            dve.wait_ge(max_placed, q * 8 + (pair + 1))
            nc.vector.tensor_reduce(neg_max[:, g % 2, col:col + 2], psum[:, bank:bank + 2, :], AX.X, ALU.max,
                                    negate=True).then_inc(max_used, 1)

        def turn_shift(pe, q, g):
            pe.wait_ge(max_used, q * 8 + 10)
            nc.tensor.transpose(psum[0:16, MISC, 0:P], neg_max[:, g % 2, :], ident[:, :]).then_inc(shift_placed, 1)

        def keep_shift(act, q):
            act.wait_ge(shift_placed, q + 1)
            act.wait_ge(shift_loaded, q * SHIFT_DMAS * 16)
            nc.scalar.copy(shift[:, :], psum[0:16, MISC, 0:P])
            nc.scalar.copy(shift_parts[:, 0, :], psum[0:16, MISC, 0:P]).then_inc(shift_kept, 1)

        def split_shift(pool, q):
            pool.wait_ge(shift_kept, q + 1)
            nc.gpsimd.tensor_tensor(shift_rest[:, :], shift[:, :], shift_parts[:, 0, :], ALU.subtract
                                    ).then_inc(shift_step, 1)
            pool.wait_ge(shift_step, q * 2 + 1)
            pass_wait(pool)
            nc.gpsimd.tensor_copy(shift_parts[:, 1, :], shift_rest[:, :]).then_inc(shift_step, 1)
            pool.wait_ge(shift_step, q * 2 + 2)
            nc.gpsimd.tensor_tensor(shift_parts[:, 2, :], shift_rest[:, :], shift_parts[:, 1, :], ALU.subtract
                                    ).then_inc(shift_ready, 1)

        def load_shift(sp, q, g):
            sp.wait_ge(shift_ready, q + 1)
            for h in range(2):
                for part in range(3):
                    row = 64 * h + ROWS + part
                    sp.dma_start(q_ring[row:row + 1, g, :, :].rearrange("p h (t c) -> p (h t) c", c=P),
                                 shift_parts[8 * h:8 * h + 8, part, :]).then_inc(shift_loaded, 16)

        def score_tile(pe, q, g, u):
            tile, head = divmod(u, 4)
            r, h = 64 * (head % 2), head // 2
            if u == 0:
                pe.wait_ge(shift_loaded, (q + 1) * SHIFT_DMAS * 16)
            pe.wait_ge(exp_done, q * 16 + (u + 1))
            nc.tensor.matmul(psum[:, SCORE + u % 2, :], k_ring[r:r + ROWS + 3, g, h, tile * P:(tile + 1) * P],
                             q_ring[r:r + ROWS + 3, g, h, :], start=True, stop=True).then_inc(score_placed, 1)

        def exponential(act, q, u):
            act.wait_ge(score_placed, q * 16 + (u + 1))
            nc.scalar.activation(probs[:, u // 4, u % 4, :], psum[:, SCORE + u % 2, :], ACT.Exp, scale=SCALE
                                 ).then_inc(exp_done, 1)

        def weigh(pe, q, g, tile):
            pe.wait_ge(exp_done, q * 16 + (tile * 4 + 6))
            if tile == 0:
                pe.wait_ge(v_filled, q + 1)
                pe.wait_ge(o_kept, q)
            for head in range(4):
                i = nc.tensor.matmul(psum[32 * head:32 * head + 32, OUT_T, :], v_ring[:, g, tile, head, :],
                                     probs[:, tile, head, :], start=tile == 0, stop=tile == TT - 1,
                                     skip_group_check=True)
            if tile == TT - 1:
                i.then_inc(o_placed, 1)

        def keep_sums(act, q):
            act.wait_ge(o_placed, q + 1)
            nc.scalar.copy(out_t[:, :], psum[:, OUT_T, :]).then_inc(o_kept, 1)

        def turn_sums(pe, q):
            pe.wait_ge(o_kept, q + 1)
            for t in range(TT):
                i = nc.tensor.transpose(psum[:, MISC, t * P:(t + 1) * P], out_t[:, t * P:(t + 1) * P], ident[:, :])
            i.then_inc(o_turned, 1)

        def divide(dve, q, g):
            sums = psum[:, MISC, :].rearrange("p (t h c) -> p t h c", t=TT, h=4)
            dve.wait_ge(o_turned, q + 1)
            nc.vector.reciprocal(weight[:, :, :], sums[:, :, :, HEAD_DIM]).then_inc(weight_ready, 1)
            dve.wait_ge(weight_ready, q + 1)
            nc.vector.tensor_tensor(
                attended[:, :, 32 * g:32 * g + 32].rearrange("p t (h d) -> p t h d", h=4), sums[:, :, :, 0:HEAD_DIM],
                weight[:, :, :].unsqueeze(3).broadcast_to([P, TT, 4, HEAD_DIM]), ALU.mult).then_inc(attended_ready, 1)

        def load_residual(sp, b):
            sp.wait_ge(x2_ready, b)
            sp.dma_start(residual[:, :, :], x1[bass.ds(b * SEQ, SEQ), :].rearrange("(t p) d -> p t d", p=P)
                         ).then_inc(residual_loaded, 16)

        def add_residual(dve, b):
            dve.wait_ge(residual_loaded, (b + 1) * 16)
            dve.wait_ge(attended_ready, b * 4 + 5)
            dve.wait_ge(dispatched[0], b * (16 * TT) + 16 * TT * BATCH // 2)
            dve.wait_ge(x2_passed, b * 16 + 16)
            nc.vector.tensor_tensor(stage[:, 0, :, 0:D], residual[:, :, :], attended[:, :, :], ALU.add
                                    ).then_inc(x2_ready, 1)
            dve.wait_ge(x2_ready, b + 1)

        def pass_x2(sp, b):
            sp.wait_ge(x2_ready, b + 1)
            sp.dma_start(out[bass.ds(b * SEQ, SEQ), :].rearrange("(t p) d -> p t d", p=P), stage[:, 0, :, 0:D]
                         ).then_inc(x2_passed, 16)

        def pe_batch(pe, b, below, prep, follows):
            for g in range(QUADS):
                q = b * 4 + g
                for u in range(16):
                    score_tile(pe, q, g, u)
                    if g < 2 or follows:
                        if u == 0:
                            pe.wait_ge(quad_loaded[(g + 2) % 4], (b + (1 + (g + 2) // 4)) * 64)
                        max_tile(pe, q + 2, (g + 2) % 4, u)
                    if u == 2 and (g < 3 or follows):
                        pe.wait_ge(attended_ready, q)
                        if g == 2:
                            pe.wait_ge(below_ready, b + BATCH)
                            if prep:
                                pe.wait_ge(proj_kept, b * 4 + 10)
                        if g == 3:
                            pe.wait_ge(route_ready, b + BATCH)
                            if prep:
                                pe.wait_ge(v_kept, b + 3)
                        turn_shift(pe, q + 1, (g + 1) % 4)
                    if u == 3 or u == 7 or u == 11 or u == 15:
                        tile = (u // 4 + 3) % 4
                        if tile < 3:
                            weigh(pe, q, g, tile)
                        elif g > 0:
                            weigh(pe, q - 1, g - 1, tile)
                        elif below is not None:
                            weigh(pe, below * 4 + 3, 3, tile)
                    if u == 6:
                        if g < 3 or follows:
                            pe.wait_ge(shift_kept, q + 2)
                        if g == 1 and prep:
                            pe.wait_ge(prep_xn_t_ready, b + 3)
                        if g == 2 and prep:
                            pe.wait_ge(proj_kept, b * 4 + 11)
                        if g == 3 and not follows:
                            pe.wait_ge(route_ready, b + BATCH)
                        if g > 0:
                            turn_sums(pe, q - 1)
                        elif below is not None:
                            turn_sums(pe, below * 4 + 3)
                    if prep:
                        if (g, u) == (1, 4):
                            pe.wait_ge(shift_kept, q + 2)
                            prep_turn(pe, b + 2)
                        if (g, u) == (1, 14):
                            pe.wait_ge(attended_ready, q + 1)
                            pe.wait_ge(below_ready, b + BATCH)
                            project(pe, b + 2, 0)
                        if (g, u) == (2, 0):
                            pe.wait_ge(proj_kept, b * 4 + 9)
                            project(pe, b + 2, 1)
                        if (g, u) == (2, 4):
                            pe.wait_ge(shift_kept, q + 2)
                            project(pe, b + 2, 2)
                        if (g, u) == (2, 8):
                            pe.wait_ge(attended_ready, q + 1)
                            project(pe, b + 2, 3)
                        if (g, u) == (2, 10):
                            pe.wait_ge(proj_kept, b * 4 + 12)
                            project_v(pe, b + 2)
                    if (g, u) == (1, 8) and below is not None:
                        pe.wait_ge(attended_ready, q + 1)
                        turn_tokens(pe, below + BATCH, 0, MISC)
                    if (g, u) == (1, 10) and below is not None:
                        gate_logits(pe, below + BATCH, 0, MISC)
                    if (g, u) == (2, 12) and below is not None:
                        pe.wait_ge(attended_ready, q + 1)
                        if prep:
                            pe.wait_ge(v_kept, b + 3)
                        count_places(pe, below + BATCH, MISC)

        def act_batch(act, b, below, prep, follows):
            for g in range(QUADS):
                q = b * 4 + g
                for u in range(16):
                    exponential(act, q, u)
                    if u == 4 and (g < 3 or follows):
                        keep_shift(act, q + 1)
                    if u == 5:
                        if g > 0:
                            keep_sums(act, q - 1)
                        elif below is not None:
                            keep_sums(act, below * 4 + 3)
                    if prep:
                        if (g, u) == (1, 6):
                            prep_keep_turned(act, b + 2)
                        if (g, u) == (1, 15):
                            keep_projection(act, b + 2, 0)
                        if (g, u) == (2, 1):
                            keep_projection(act, b + 2, 1)
                        if (g, u) == (2, 5):
                            keep_projection(act, b + 2, 2)
                        if (g, u) == (2, 9):
                            keep_projection(act, b + 2, 3)
                        if (g, u) == (2, 11):
                            keep_v(act, b + 2)
                        if (g, u) == (2, 13):
                            keep_first_part(act, b + 2, 0)
                        if (g, u) == (2, 15):
                            keep_second_part(act, b + 2, 0)
                        if (g, u) == (3, 6):
                            keep_first_part(act, b + 2, 1)
                        if (g, u) == (3, 9):
                            keep_second_part(act, b + 2, 1)
                    if (g, u) == (1, 9) and below is not None:
                        keep_turned(act, below + BATCH, 0, MISC)
                    if (g, u) == (2, 0) and below is not None:
                        gate_exponentials(act, below + BATCH)

        def dve_batch(dve, b, below, prep, follows):
            r = None if below is None else below + BATCH
            for g in range(QUADS):
                q = b * 4 + g
                for pair in range(8):
                    if g < 2 or follows:
                        take_max(dve, q + 2, (g + 2) % 4, pair)
                    if (g, pair) == (0, 0) and prep:
                        prep_measure(dve, b + 2)
                    if pair == 3:
                        if g > 0:
                            divide(dve, q - 1, g - 1)
                        elif below is not None:
                            divide(dve, below * 4 + 3, 3)
                            add_residual(dve, below)
                            measure(dve, Steps(dve, route_step, route_start(r)), 0)
                    if (g, pair) == (1, 1) and below is not None:
                        normalize(dve, r, 0)
                    if (g, pair) == (1, 5) and below is not None:
                        choose(dve, Steps(dve, route_step, route_start(r) + 2), r, MISC)
                    if (g, pair) == (2, 7) and below is not None:
                        route(dve, Steps(dve, route_step, route_start(r) + 7), r, 0, MISC, below)

        def pool_batch(pool, b, below, prep, follows):
            r = None if below is None else below + BATCH
            for g in range(QUADS):
                q = b * 4 + g
                if g < 3 or follows:
                    split_shift(pool, q + 1)
                if g == 0 or follows:
                    if g > 0:
                        pool.wait_ge(o_placed, q)
                        fill_v(pool, b + 1, g - 1, q + 3)
                    elif below is not None:
                        pool.wait_ge(o_placed, q)
                        fill_v(pool, b, 3, q + 3)
                if g == 0:
                    if prep:
                        prep_normalize(pool, b + 2)
                    if below is not None:
                        invert_deviation(pool, r)
                if g == 2 and prep:
                    rotate(pool, b + 2, 0)
                    take_rest(pool, b + 2, 0)
                    rotate(pool, b + 2, 1)
                    keep_third_part(pool, b + 2, 0)
                if g == 3:
                    if prep:
                        take_rest(pool, b + 2, 1)
                        keep_third_part(pool, b + 2, 1)
                    if below is not None:
                        scatter_tokens(pool, r, 0, 1)

        def sp_batch(sp, b, below, prep, follows):
            for g in range(QUADS):
                q = b * 4 + g
                if g == 0 and prep:
                    load_prep(sp, b + 2)
                if g == 0 or follows:
                    sp.wait_ge(score_placed, q * 16)
                    pass_wait(sp)
                    load_quad(sp, b + (g > 0), (g + 3) % 4)
                if g < 3 or follows:
                    load_shift(sp, q + 1, (g + 1) % 4)
                if g == 0 and below is not None:
                    pass_x2(sp, below)
                if g == 1:
                    load_residual(sp, b)
                if g == 3 and prep:
                    for c in range(2):
                        write_parts(sp, b + 2, c)

        def route_all(eng, body):
            with eng.Fori(0, BATCH // 2 - 1) as i:
                for s in range(2):
                    body(i * 2 + s, i, s, False)
            for s in range(2):
                body(BATCH - 2 + s, BATCH // 2 - 1, s, s == 1)

        def route_start(r):
            return r * ROUTE_STEPS + 2

        def attend_all(eng, body):
            body(eng, 0, None, True, True)
            with eng.Fori(0, BATCH - 3) as below:
                body(eng, below + 1, below, True, True)
            body(eng, BATCH - 2, BATCH - 3, False, True)
            body(eng, BATCH - 1, BATCH - 2, False, False)

        LAST_QUAD = BATCH * QUADS - 1
        LAST_ROUTED = 2 * BATCH - 1

        @block.sync
        def _(sp):
            loads = [(ident[:, :], identity), (counters[:, :, :], count_mats), (iota_e[:, :], expert_iota[0]),
                     (iota_low[:, :], expert_iota[1]), (numbers[:, :], token_number), (wg_sb[:, :], wg),
                     (wq_sb[:, :, :], wq_t), (wk_sb[:, :, :], wk_t), (wv_sb[:, :], wv_t), (bias_sb[:, :], qk_bias),
                     (v_bias_sb[:, :], v_bias.broadcast_to([P, D])), (rope_sb[:, :, :], rope)]
            assert len(loads) == CONSTS
            for dst, src in loads:
                sp.dma_start(dst, src).then_inc(consts_loaded, 16)
            sp.wait_ge(empty_ready, 3)
            for k in range(2):
                sp.dma_start(slots[k].rearrange("(n p) c -> p n c", p=P),
                             empty[:, :].unsqueeze(1).broadcast_to([P, TOKENS // P, ROW])).then_inc(slots_cleared, 16)
            with sp.Fori(0, BATCH // 2) as i:
                for s in range(2):
                    b = i * 2 + s
                    sp.wait_ge(dispatched[s], i * (16 * TT))
                    sp.dma_start(stage[:, s, :, 0:D], x[bass.ds(b * SEQ, SEQ), :].rearrange("(t p) d -> p t d", p=P)
                                 ).then_inc(x_loaded[s], 16)
            sp.dma_start(x1, x).then_inc(x_passed, 16)
            for e in range(0, EXPERTS, 4):
                sp.dma_start(w2_sb[:, e:e + 4, :, :], w2[e:e + 4].rearrange("e (c p) d -> p e c d", p=P)
                             ).then_inc(w2_loaded, 16)
            for k in range(UNROLL):
                load_w1(sp, 0, 0, k)
            load_experts(sp, 0)
            for k in range(UNROLL):
                load_w1(sp, 1, 0, k)
            for k in range(UNROLL):
                sp.wait_ge(rows_written[k], 16 * ST * (EXPERTS // UNROLL))
            with sp.Fori(0, 2) as n:
                load_prep(sp, n)
                for c in range(2):
                    write_parts(sp, n, c)
            for g in range(3):
                load_quad(sp, 0, g)
            load_shift(sp, 0, 0)
            attend_all(sp, sp_batch)
            pass_x2(sp, BATCH - 1)
            load_experts(sp, 1)
            for k in range(UNROLL):
                sp.wait_ge(rows_written[k], 2 * 16 * ST * (EXPERTS // UNROLL))

        @block.gpsimd
        def _(pool):
            nc.gpsimd.memset(minus_half[:, :], -0.5).then_inc(empty_ready, 1)
            nc.gpsimd.memset(empty[:, :], 0.0).then_inc(empty_ready, 1)
            pool.wait_ge(empty_ready, 2)
            nc.gpsimd.memset(empty[:, D:D + 1].bitcast(I32), NOWHERE).then_inc(empty_ready, 1)
            nc.gpsimd.memset(k_ring[:, :, :, :], 1.0)
            nc.gpsimd.memset(v_ring[:, :, :, :, :], 0.0).then_inc(ring_cleared, 1)
            pool.wait_ge(ring_cleared, 1)
            nc.gpsimd.memset(v_ring[:, :, :, :, HEAD_DIM:HEAD_DIM + 1], 1.0).then_inc(ring_cleared, 1)
            pool.wait_ge(ring_cleared, 2)
            pool.wait_ge(slots_cleared, 32)

            def body(b, i, s, last):
                if not last:
                    invert_deviation(pool, b + 1)
                scatter_tokens(pool, b, s, 0)
            invert_deviation(pool, 0)
            route_all(pool, body)
            pool.wait_ge(x_passed, 16)
            pool_experts(pool, 0)
            with pool.Fori(0, 2) as n:
                prep_normalize(pool, n)
                for c in range(2):
                    rotate(pool, n, c)
                    take_rest(pool, n, c)
                    keep_third_part(pool, n, c)
            for g in range(QUADS):
                fill_v(pool, 0, g, g)
            split_shift(pool, 0)
            attend_all(pool, pool_batch)
            invert_deviation(pool, LAST_ROUTED)
            scatter_tokens(pool, LAST_ROUTED, 0, 1)
            pool.wait_ge(x2_passed, 16 + 16 * BATCH)
            pool_experts(pool, 1)

        @block.vector
        def _(dve):
            nc.vector.memset(carry[:, :], 0.0).then_inc(route_step, 1)
            dve.wait_ge(consts_loaded, 16 * CONSTS)

            def measure_staged(steps, i, s):
                dve.wait_ge(x_loaded[s], (i + 1) * 16)
                measure(dve, steps, s)

            def body(b, i, s, last):
                steps = Steps(dve, route_step, b * ROUTE_STEPS + 3)
                if not last:
                    measure_staged(steps, i + s, 1 - s)
                choose(dve, steps, b, 2 + s)
                if not last:
                    normalize(dve, b + 1, 1 - s)
                route(dve, steps, b, s, 2 + s, b)
                assert last or steps.n == ROUTE_STEPS
            measure_staged(Steps(dve, route_step, 1), 0, 0)
            normalize(dve, 0, 0)
            route_all(dve, body)
            nc.vector.memset(carry[:, :], 0.0).then_inc(route_step, 1)
            dve_experts(dve, 0)
            with dve.Fori(0, 2) as n:
                prep_measure(dve, n)
            for g in range(2):
                for pair in range(8):
                    take_max(dve, g, g, pair)
            attend_all(dve, dve_batch)
            divide(dve, LAST_QUAD, QUADS - 1)
            add_residual(dve, BATCH - 1)
            steps = Steps(dve, route_step, route_start(LAST_ROUTED))
            measure(dve, steps, 0)
            normalize(dve, LAST_ROUTED, 0)
            choose(dve, steps, LAST_ROUTED, MISC)
            route(dve, steps, LAST_ROUTED, 0, MISC, BATCH - 1)
            dve_experts(dve, 1)

        @block.scalar
        def _(act):
            act.sem_inc(y_used, UNROLL)
            act.sem_inc(w1_used, UNROLL)
            act.sem_inc(roped, 2)
            act.sem_inc(max_used, 2)
            act.sem_inc(exp_done, 2)
            act.sem_inc(attended_ready, 1)
            act.sem_inc(x2_passed, 16)
            act.wait_ge(consts_loaded, 16 * CONSTS)

            def body(b, i, s, last):
                gate_exponentials(act, b)
                if not last:
                    keep_turned(act, b + 1, 1 - s, 1 - s)
            keep_turned(act, 0, 0, 0)
            route_all(act, body)
            act_experts(act, 0)
            with act.Fori(0, 2) as n:
                prep_keep_turned(act, n)
                for c in range(4):
                    keep_projection(act, n, c)
                keep_v(act, n)
                for c in range(2):
                    keep_first_part(act, n, c)
                    keep_second_part(act, n, c)
            keep_shift(act, 0)
            attend_all(act, act_batch)
            keep_sums(act, LAST_QUAD)
            keep_turned(act, LAST_ROUTED, 0, MISC)
            gate_exponentials(act, LAST_ROUTED)
            act_experts(act, 1)

        @block.tensor
        def _(pe):
            pe.wait_ge(consts_loaded, 16 * CONSTS)

            def body(b, i, s, last):
                gate_logits(pe, b, s, 2 + s)
                if not last:
                    turn_tokens(pe, b + 1, 1 - s, 1 - s)
                count_places(pe, b, 2 + s)
            turn_tokens(pe, 0, 0, 0)
            route_all(pe, body)
            pe.wait_ge(w2_loaded, 16 * 4)
            pe_experts(pe, 0)
            with pe.Fori(0, 2) as n:
                pe.wait_ge(v_kept, n)
                prep_turn(pe, n)
                for c in range(4):
                    pe.wait_ge(proj_kept, n * 4 + c)
                    project(pe, n, c)
                pe.wait_ge(proj_kept, n * 4 + 4)
                project_v(pe, n)
            pe.wait_ge(ring_cleared, 2)
            for g in range(2):
                pe.wait_ge(quad_loaded[g], 64)
                for w in range(16):
                    max_tile(pe, g, g, w)
            pe.wait_ge(v_kept, 2)
            turn_shift(pe, 0, 0)
            attend_all(pe, pe_batch)
            weigh(pe, LAST_QUAD, QUADS - 1, TT - 1)
            pe.wait_ge(attended_ready, LAST_QUAD + 1)
            turn_sums(pe, LAST_QUAD)
            pe.wait_ge(attended_ready, LAST_QUAD + 2)
            turn_tokens(pe, LAST_ROUTED, 0, MISC)
            gate_logits(pe, LAST_ROUTED, 0, MISC)
            count_places(pe, LAST_ROUTED, MISC)
            pe_experts(pe, 1)


def kernel(L0_attn_x, L0_attn_wq_w, L0_attn_wq_b, L0_attn_wk_w, L0_attn_wk_b, L0_attn_wv_w, L0_attn_wv_b,
           L0_ffn_Wg, L0_ffn_w1, L0_ffn_w2):
    import ml_dtypes
    import numpy as np
    import concourse.bacc as bacc
    from concourse.bass_utils import run_bass_kernel_spmd

    quad, par, feat, pair = np.meshgrid(np.arange(QUADS), np.arange(2), np.arange(HEAD_DIM), np.arange(2),
                                        indexing="ij")
    order = ((4 * quad + 2 * pair + par) * HEAD_DIM + feat).reshape(-1)
    partner = order ^ 1
    feature = feat.reshape(-1)

    theta = np.float32(10000.0) ** (np.float32(-2.0) * np.arange(HEAD_DIM // 2, dtype=np.float32)
                                    / np.float32(HEAD_DIM))
    angle = np.outer(np.arange(SEQ, dtype=np.float32), theta.astype(np.float32)).astype(np.float32)
    cosine = np.cos(angle).T[feature // 2]
    sine = np.sin(angle).T[feature // 2] * np.where(feature % 2 == 0, -1.0, 1.0)[:, None]

    a = np.asarray
    arrays = {
        "x": a(L0_attn_x).reshape(TOKENS, D),
        "wq_t": np.stack([a(L0_attn_wq_w)[order].T, a(L0_attn_wq_w)[partner].T], axis=1),
        "wk_t": np.stack([a(L0_attn_wk_w)[order].T, a(L0_attn_wk_w)[partner].T], axis=1),
        "wv_t": a(L0_attn_wv_w).T,
        "qk_bias": np.stack([a(L0_attn_wq_b)[order], a(L0_attn_wq_b)[partner],
                             a(L0_attn_wk_b)[order], a(L0_attn_wk_b)[partner]], axis=1),
        "v_bias": a(L0_attn_wv_b).reshape(1, D),
        "wg": a(L0_ffn_Wg),
        "w1": a(L0_ffn_w1),
        "w2": a(L0_ffn_w2),
        "rope": np.stack([cosine, sine], axis=1).astype(np.float32),
        "identity": np.eye(P, dtype=np.float32),
        "count_mats": np.stack([np.triu(np.ones((P, P)), 1), np.ones((P, P))], axis=1).astype(ml_dtypes.bfloat16),
        "expert_iota": np.stack([np.tile(np.arange(EXPERTS), (P, 1)), np.tile(np.arange(EXPERTS) - EXPERTS, (P, 1))]
                                ).astype(np.float32),
        "token_number": np.arange(TOKENS, dtype=np.int32).reshape(-1, P).T,
    }
    arrays = {name: np.ascontiguousarray(v) for name, v in arrays.items()}
    nc = bacc.Bacc("TRN2", target_bir_lowering=False, num_devices=1)
    args = [nc.dram_tensor(name, v.shape, mybir.dt.from_np(v.dtype), kind="ExternalInput").ap()
            for name, v in arrays.items()]
    out = nc.dram_tensor("out", (TOKENS, D), F32, kind="ExternalOutput").ap()
    macaron_block_kernel(nc, *args, out)
    r = run_bass_kernel_spmd(nc, [arrays], core_ids=[0])
    return r.results[0]["out"].reshape(BATCH, SEQ, D)
```

```python
from contextlib import ExitStack, nullcontext

import concourse.bass as bass
from concourse import mybir

ALU = mybir.AluOpType
ACT = mybir.ActivationFunctionType
AX = mybir.AxisListType
F32 = mybir.dt.float32
BF16 = mybir.dt.bfloat16
I32 = mybir.dt.int32
U32 = mybir.dt.uint32

P = 128
BATCH, SEQ, D = 8, 512, 128
TOKENS = BATCH * SEQ
TT = SEQ // P
EXPERTS, HID = 16, 512
CAP = TOKENS // EXPERTS
ST = CAP // P
FC = HID // P
ROW = D + 2
EPS = 1e-5
NOWHERE = 1 << 20
UNROLL = 4


class Steps:

    def __init__(self, eng, sem, start=0):
        self.eng, self.sem, self.start, self.n = eng, sem, start, 0

    def did(self, instruction):
        instruction.then_inc(self.sem, 1)
        self.n += 1

    def settle(self):
        self.eng.wait_ge(self.sem, self.start + self.n)
ROUTE_STEPS = 16
CONSTS = 12
HEADS, HEAD_DIM = 16, 8
QUADS = HEADS // 4
Q_PARTS = (0, 0, 0, 1, 1, 2)
K_PARTS = (0, 1, 2, 0, 1, 0)
SLOTS = len(Q_PARTS)
PART_SLOTS = (((0, 2, 1, 0), (3, 4, 1, 1), (5, 5, 1, 2)),
              ((0, 3, 3, 0), (5, 5, 1, 0), (1, 4, 3, 1), (2, 2, 1, 2)))
ROWS = SLOTS * HEAD_DIM
SHIFT_ROW = 64 + ROWS
SHIFT_DMAS = 3


def macaron_block_kernel(nc, x, wq_t, wk_t, wv_t, qk_bias, v_bias, wg, w1, w2, rope, identity, count_mats,
                         expert_iota, token_number, out):
    SCALE = 1.0 / float(HEAD_DIM) ** 0.5

    with ExitStack() as ctx:
        def sb(name, shape, dt):
            return ctx.enter_context(nc.sbuf_tensor(name, shape, dt))

        def sem(name):
            return ctx.enter_context(nc.semaphore(name))

        x1 = nc.dram_tensor("x1", (TOKENS, D), F32).ap()
        slots = [nc.dram_tensor(f"slots{k}", (TOKENS, ROW), F32).ap() for k in range(2)]
        rows_of = [x1, out]

        ident = sb("ident", [P, P], F32)
        counters = sb("counters", [P, 2, P], BF16)
        iota_e = sb("iota_e", [P, EXPERTS], F32)
        iota_low = sb("iota_low", [P, EXPERTS], F32)
        numbers = sb("numbers", [P, TOKENS // P], I32)
        wg_sb = sb("wg_sb", [P, EXPERTS], F32)
        w2_sb = sb("w2_sb", [P, EXPERTS, FC, D], F32)
        w1_ring = sb("w1_ring", [P, UNROLL, HID], F32)
        empty = sb("empty", [P, ROW], F32)

        stage = sb("stage", [P, 2, TT, ROW], F32)
        xn = sb("xn", [P, 2, TT, D], F32)
        xn_t = sb("xn_t", [P, 2, SEQ], F32)
        stats = sb("stats", [P, TT, 6], F32)
        moments = sb("moments", [P, TT, 2], F32)
        minus_half = sb("minus_half", [P, TT], F32)
        spread = sb("spread", [P, TT], F32)
        rstd = sb("rstd", [P, TT], F32)
        top = sb("top", [P, TT], F32)
        below = sb("below", [P, TT, EXPERTS], F32)
        tied = sb("tied", [P, TT, EXPERTS], F32)
        first = sb("first", [P, TT], F32)
        onehot = sb("onehot", [P, TT, EXPERTS], BF16)
        gate_exp = sb("gate_exp", [P, TT, EXPERTS], F32)
        place = sb("place", [P, TT, EXPERTS], F32)
        carry = sb("carry", [P, EXPERTS], F32)
        loc = sb("loc", [P, TT], F32)
        base = sb("base", [P, TT], F32)
        over = sb("over", [P, TT], F32)
        half = sb("half", [P, TT], F32)
        gate_sum = sb("gate_sum", [P, TT], F32)
        dest = sb("dest", [P, 2, TT], I32)

        slot_rows = sb("slot_rows", [P, UNROLL, ST, ROW], F32)
        new_rows = sb("new_rows", [P, UNROLL, ST, ROW], F32)
        slot_stats = sb("slot_stats", [P, ST, 6], F32)
        slot_moments = sb("slot_moments", [P, 2, ST, 2], F32)
        slot_spread = sb("slot_spread", [P, 2, ST], F32)
        slot_rstd = sb("slot_rstd", [P, 2, ST], F32)
        slot_xn = sb("slot_xn", [P, 2, ST, D], F32)
        slot_xn_t = sb("slot_xn_t", [P, 2, CAP], F32)
        hidden = sb("hidden", [P, 2, FC, CAP], F32)

        psum = ctx.enter_context(nc.psum_tensor("psum", [P, 8, 512], F32))

        consts_loaded = sem("consts_loaded")
        w2_loaded = sem("w2_loaded")
        x_passed = sem("x_passed")
        x_loaded = [sem(f"x_loaded{s}") for s in range(2)]
        empty_ready = sem("empty_ready")
        waits_passed = sem("waits_passed")
        slots_cleared = sem("slots_cleared")
        w1_loaded = [sem(f"w1_loaded{k}") for k in range(UNROLL)]
        w1_used = sem("w1_used")
        slots_loaded = [sem(f"slots_loaded{k}") for k in range(UNROLL)]
        rows_written = [sem(f"rows_written{k}") for k in range(UNROLL)]
        dispatched = [sem(f"dispatched{s}") for s in range(2)]
        xn_ready = sem("xn_ready")
        xn_t_placed = sem("xn_t_placed")
        xn_t_ready = sem("xn_t_ready")
        logits_ready = sem("logits_ready")
        below_ready = sem("below_ready")
        gate_exp_ready = sem("gate_exp_ready")
        onehot_ready = sem("onehot_ready")
        place_ready = sem("place_ready")
        route_ready = sem("route_ready")
        route_step = sem("route_step")
        moments_ready = sem("moments_ready")
        rstd_ready = sem("rstd_ready")
        slot_stats_ready = sem("slot_stats_ready")
        slot_moments_ready = sem("slot_moments_ready")
        slot_rstd_ready = sem("slot_rstd_ready")
        slot_xn_ready = sem("slot_xn_ready")
        slot_xn_t_placed = sem("slot_xn_t_placed")
        slot_xn_t_ready = sem("slot_xn_t_ready")
        hidden_placed = sem("hidden_placed")
        hidden_ready = sem("hidden_ready")
        y_placed = sem("y_placed")
        y_used = sem("y_used")

        wq_sb = sb("wq_sb", [P, 2, D], F32)
        wk_sb = sb("wk_sb", [P, 2, D], F32)
        wv_sb = sb("wv_sb", [P, D], F32)
        bias_sb = sb("bias_sb", [P, 4], F32)
        v_bias_sb = sb("v_bias_sb", [P, D], F32)
        rope_sb = sb("rope_sb", [P, 2, SEQ], F32)
        prep_x = sb("prep_x", [P, TT, D], F32)
        prep_stats = sb("prep_stats", [P, TT, 6], F32)
        prep_moments = sb("prep_moments", [P, TT, 2], F32)
        prep_spread = sb("prep_spread", [P, TT], F32)
        prep_rstd = sb("prep_rstd", [P, TT], F32)
        prep_xn = sb("prep_xn", [P, TT, D], F32)
        prep_xn_t = sb("prep_xn_t", [P, SEQ], F32)
        proj = sb("proj", [P, 4, SEQ], F32)
        turned = sb("turned", [P, 2, SEQ], F32)
        parts = sb("parts", [P, 2, 3, SEQ], BF16)
        v_flat = sb("v_flat", [P, BATCH, TT, D], F32)
        v_ring = sb("v_ring", [P, QUADS, TT, 4, 32], F32)
        q_ring = sb("q_ring", [P, QUADS, 2, 2, SEQ], BF16)
        k_ring = sb("k_ring", [P, QUADS, 2, SEQ], BF16)
        neg_max = sb("neg_max", [P, 2, 16], F32)
        shift = sb("shift", [16, P], F32)
        shift_rest = sb("shift_rest", [16, P], F32)
        shift_parts = sb("shift_parts", [16, 3, P], BF16)
        probs = sb("probs", [P, TT, 4, SEQ], F32)
        out_t = sb("out_t", [P, SEQ], F32)
        weight = sb("weight", [P, TT, 4], F32)
        attended = sb("attended", [P, TT, D], F32)
        residual = sb("residual", [P, TT, D], F32)
        qk_rows = nc.dram_tensor("qk_rows", (BATCH, 2, SLOTS, P, SEQ), BF16).ap()

        prep_x_loaded = sem("prep_x_loaded")
        prep_stats_ready = sem("prep_stats_ready")
        prep_moments_ready = sem("prep_moments_ready")
        prep_rstd_ready = sem("prep_rstd_ready")
        prep_xn_ready = sem("prep_xn_ready")
        v_filled = sem("v_filled")
        ring_cleared = sem("ring_cleared")
        rope_step = sem("rope_step")
        roped = sem("roped")
        first_part_ready = sem("first_part_ready")
        rest_ready = sem("rest_ready")
        second_part_ready = sem("second_part_ready")
        parts_ready = sem("parts_ready")
        parts_written = [sem(f"parts_written{c}") for c in range(2)]
        quad_loaded = [sem(f"quad_loaded{g}") for g in range(QUADS)]
        shift_loaded = sem("shift_loaded")
        max_placed = sem("max_placed")
        max_used = sem("max_used")
        shift_first = sem("shift_first")
        shift_step = sem("shift_step")
        shift_ready = sem("shift_ready")
        ring_placed = sem("ring_placed")
        ring_used = sem("ring_used")
        o_placed = sem("o_placed")
        o_kept = sem("o_kept")
        o_turned = sem("o_turned")
        weight_ready = sem("weight_ready")
        attended_ready = sem("attended_ready")
        residual_loaded = sem("residual_loaded")
        x2_ready = sem("x2_ready")
        x2_passed = sem("x2_passed")

        block = ctx.enter_context(nc.Block())


        def pass_wait(eng):
            eng.sem_inc(waits_passed, 1)

        def measure(dve, steps, s):
            for t in range(TT):
                i = nc.vector.bn_stats(stats[:, t, :], stage[:, s, t, 0:D])
            steps.did(i)
            steps.settle()
            pass_wait(dve)
            for t in range(TT):
                i = nc.vector.bn_aggr(moments[:, t, :], stats[:, t, :])
            steps.did(i)
            steps.settle()
            nc.vector.tensor_scalar(spread[:, :], moments[:, :, 1], EPS, None, ALU.add).then_inc(moments_ready, 1)

        def invert_deviation(pool, r):
            pool.wait_ge(moments_ready, r + 1)
            nc.gpsimd.tensor_tensor(rstd[:, :], spread[:, :], minus_half[:, :], ALU.pow).then_inc(rstd_ready, 1)

        def normalize(dve, r, s):
            dve.wait_ge(rstd_ready, r + 1)
            for t in range(TT):
                i = nc.vector.tensor_scalar(xn[:, s, t, :], stage[:, s, t, 0:D], moments[:, t, 0:1],
                                            rstd[:, t:t + 1], ALU.subtract, ALU.mult)
            i.then_inc(xn_ready, 1)

        def choose(dve, steps, r, bank):
            logits = psum[:, bank, 0:TT * EXPERTS].rearrange("p (t e) -> p t e", e=EXPERTS)
            dve.wait_ge(logits_ready, r + 1)
            steps.did(nc.vector.tensor_reduce(top[:, :], logits, AX.X, ALU.max))
            steps.settle()
            nc.vector.tensor_tensor(below[:, :, :], logits, top[:, :].unsqueeze(2).broadcast_to([P, TT, EXPERTS]),
                                    ALU.subtract).then_inc(below_ready, 1)
            dve.wait_ge(below_ready, r + 1)
            steps.did(nc.vector.tensor_scalar(tied[:, :, :], below[:, :, :], 0.0, -float(EXPERTS),
                                              ALU.is_ge, ALU.mult))
            steps.settle()
            steps.did(nc.vector.tensor_tensor(tied[:, :, :], tied[:, :, :],
                                              iota_e[:, :].unsqueeze(1).broadcast_to([P, TT, EXPERTS]), ALU.add))
            steps.settle()
            steps.did(nc.vector.tensor_reduce(first[:, :], tied[:, :, :], AX.X, ALU.min))
            steps.settle()
            nc.vector.tensor_tensor(onehot[:, :, :], iota_low[:, :].unsqueeze(1).broadcast_to([P, TT, EXPERTS]),
                                    first[:, :].unsqueeze(2).broadcast_to([P, TT, EXPERTS]),
                                    ALU.is_equal).then_inc(onehot_ready, 1)
            steps.did(nc.vector.tensor_scalar(base[:, :], first[:, :], float(EXPERTS), float(CAP),
                                              ALU.add, ALU.mult))

        def route(dve, steps, r, s, bank, b):
            earlier = psum[:, bank, 64:64 + TT * EXPERTS].rearrange("p (t e) -> p t e", e=EXPERTS)
            total = psum[:, bank, 128:128 + EXPERTS]
            dve.wait_ge(place_ready, r + 1)
            dve.wait_ge(onehot_ready, r + 1)
            steps.did(nc.vector.tensor_tensor(place[:, :, :], earlier,
                                              carry[:, :].unsqueeze(1).broadcast_to([P, TT, EXPERTS]), ALU.add))
            steps.settle()
            steps.did(nc.vector.tensor_tensor(place[:, :, :], place[:, :, :], onehot[:, :, :], ALU.mult))
            steps.did(nc.vector.tensor_tensor(carry[:, :], total, carry[:, :], ALU.add))
            steps.settle()
            steps.did(nc.vector.tensor_reduce(loc[:, :], place[:, :, :], AX.X, ALU.add))
            dve.wait_ge(gate_exp_ready, r + 1)
            steps.did(nc.vector.tensor_reduce(gate_sum[:, :], gate_exp[:, :, :], AX.X, ALU.add))
            steps.settle()
            steps.did(nc.vector.tensor_tensor(base[:, :], base[:, :], loc[:, :], ALU.add))
            steps.did(nc.vector.tensor_scalar(over[:, :], loc[:, :], float(CAP), float(NOWHERE), ALU.is_ge, ALU.mult))
            steps.did(nc.vector.tensor_scalar(half[:, :], loc[:, :], float(CAP), 0.5, ALU.is_lt, ALU.mult))
            steps.did(nc.vector.reciprocal(gate_sum[:, :], gate_sum[:, :]))
            steps.settle()
            nc.vector.tensor_tensor(dest[:, s, :], base[:, :], over[:, :], ALU.add)
            nc.vector.tensor_tensor(stage[:, s, :, D + 1], half[:, :], gate_sum[:, :], ALU.mult)
            nc.vector.tensor_copy(stage[:, s, :, D].bitcast(I32),
                                  numbers[:, bass.ds(b * TT, TT)]).then_inc(route_ready, 1)

        def turn_tokens(pe, r, s, bank):
            pe.wait_ge(xn_ready, r + 1)
            for t in range(TT):
                i = nc.tensor.transpose(psum[:, bank, t * P:(t + 1) * P], xn[:, s, t, :], ident[:, :])
            i.then_inc(xn_t_placed, 1)

        def gate_logits(pe, r, s, bank):
            pe.wait_ge(xn_t_ready, r + 1)
            for t in range(TT):
                i = nc.tensor.matmul(psum[:, bank, t * EXPERTS:(t + 1) * EXPERTS], xn_t[:, s, t * P:(t + 1) * P],
                                     wg_sb[:, :], start=True, stop=True)
            i.then_inc(logits_ready, 1)

        def count_places(pe, r, bank):
            pe.wait_ge(onehot_ready, r + 1)
            flat = onehot[:, :, :].rearrange("p t e -> p (t e)")
            nc.tensor.matmul(psum[:, bank, 64:64 + TT * EXPERTS], counters[:, 0, :], flat, start=True, stop=False,
                             skip_group_check=True)
            for t in range(TT - 1):
                nc.tensor.matmul(psum[:, bank, 64 + (t + 1) * EXPERTS:64 + TT * EXPERTS], counters[:, 1, :],
                                 onehot[:, t, :].unsqueeze(1).broadcast_to([P, TT - 1 - t, EXPERTS]),
                                 start=False, stop=t == TT - 2, skip_group_check=True)
            for t in range(TT):
                i = nc.tensor.matmul(psum[:, bank, 128:128 + EXPERTS], counters[:, 1, :], onehot[:, t, :],
                                     start=False, stop=t == TT - 1, skip_group_check=True)
            i.then_inc(place_ready, 1)

        def keep_turned(act, r, s, bank):
            act.wait_ge(xn_t_placed, r + 1)
            nc.scalar.copy(xn_t[:, s, :], psum[:, bank, :]).then_inc(xn_t_ready, 1)

        def gate_exponentials(act, r):
            act.wait_ge(below_ready, r + 1)
            nc.scalar.activation(gate_exp[:, :, :], below[:, :, :], ACT.Exp).then_inc(gate_exp_ready, 1)

        def scatter_tokens(pool, r, s, layer):
            pool.wait_ge(route_ready, r + 1)
            pass_wait(pool)
            for t in range(TT):
                pool.indirect_dma_start(
                    out=slots[layer][:, :],
                    out_offset=bass.IndirectOffsetOnAxis(ap=dest[:, s, t:t + 1].bitcast(U32), axis=0),
                    in_=stage[:, s, t, :], in_offset=None, bounds_check=TOKENS - 1,
                    oob_is_err=False).then_inc(dispatched[s], 16)


        def load_w1(sp, layer, i, k):
            sp.wait_ge(w1_used, i * UNROLL + (layer * EXPERTS + k + 1))
            sp.dma_start(w1_ring[:, k, :], w1[i * UNROLL + k]).then_inc(w1_loaded[k], 16)

        def load_slots(sp, layer, i, k):
            sp.wait_ge(y_used, i * UNROLL + (layer * EXPERTS + k + 1))
            sp.dma_start(slot_rows[:, k, :, :],
                         slots[layer][bass.ds((i * UNROLL + k) * CAP, CAP), :].rearrange("(s p) c -> p s c", p=P)
                         ).then_inc(slots_loaded[k], 16)

        def load_experts(sp, layer):
            for s in range(2):
                sp.wait_ge(dispatched[s], all_dispatched(s, layer))
            for k in range(UNROLL):
                load_slots(sp, layer, 0, k)
            with sp.Fori(0, EXPERTS // UNROLL - 1) as i:
                for k in range(UNROLL):
                    load_w1(sp, layer, i + 1, k)
                    load_slots(sp, layer, i + 1, k)

        def all_dispatched(s, layer):
            return 16 * TT * BATCH // 2 * (1 + 2 * layer * (s == 0))

        def measure_slots(dve, n, turn, k):
            dve.wait_ge(slots_loaded[k], (turn + 1) * 16)
            for s in range(ST):
                i = nc.vector.bn_stats(slot_stats[:, s, :], slot_rows[:, k, s, 0:D])
            i.then_inc(slot_stats_ready, 1)
            dve.wait_ge(slot_stats_ready, 2 * n + 1)
            pass_wait(dve)
            for s in range(ST):
                i = nc.vector.bn_aggr(slot_moments[:, k % 2, s, :], slot_stats[:, s, :])
            i.then_inc(slot_stats_ready, 1)
            dve.wait_ge(slot_stats_ready, 2 * n + 2)
            nc.vector.tensor_scalar(slot_spread[:, k % 2, :], slot_moments[:, k % 2, :, 1], EPS, None, ALU.add
                                    ).then_inc(slot_moments_ready, 1)

        def invert_slot_deviation(pool, n, k):
            pool.wait_ge(slot_moments_ready, n + 1)
            nc.gpsimd.tensor_tensor(slot_rstd[:, k % 2, :], slot_spread[:, k % 2, :], minus_half[:, 0:ST], ALU.pow
                                    ).then_inc(slot_rstd_ready, 1)

        def normalize_slots(dve, n, k):
            dve.wait_ge(slot_rstd_ready, n + 1)
            for s in range(ST):
                i = nc.vector.tensor_scalar(slot_xn[:, k % 2, s, :], slot_rows[:, k, s, 0:D],
                                            slot_moments[:, k % 2, s, 0:1], slot_rstd[:, k % 2, s:s + 1],
                                            ALU.subtract, ALU.mult)
            i.then_inc(slot_xn_ready, 1)

        def add_expert(dve, n, turn, k):
            dve.wait_ge(y_placed, n + 1)
            dve.wait_ge(rows_written[k], turn * (16 * ST))
            nc.vector.tensor_copy(new_rows[:, k, :, D].bitcast(I32), slot_rows[:, k, :, D].bitcast(I32))
            for s in range(ST):
                i = nc.vector.scalar_tensor_tensor(new_rows[:, k, s, 0:D], psum[:, 6 + k % 2, s * D:(s + 1) * D],
                                                   slot_rows[:, k, s, D + 1:D + 2], slot_rows[:, k, s, 0:D],
                                                   ALU.mult, ALU.add)
            i.then_inc(y_used, 1)

        def turn_slots(pe, n, k):
            pe.wait_ge(slot_xn_ready, n + 1)
            for s in range(ST):
                i = nc.tensor.transpose(psum[:, k % 2, s * P:(s + 1) * P], slot_xn[:, k % 2, s, :], ident[:, :])
            i.then_inc(slot_xn_t_placed, 1)

        def expert_in(pe, n, turn, k):
            pe.wait_ge(slot_xn_t_ready, n + 1)
            pe.wait_ge(w1_loaded[k], (turn + 1) * 16)
            for c in range(FC):
                i = nc.tensor.matmul(psum[:, 2 + 2 * (k % 2) + c // 2, (c % 2) * CAP:(c % 2 + 1) * CAP],
                                     w1_ring[:, k, c * P:(c + 1) * P], slot_xn_t[:, k % 2, :],
                                     start=True, stop=True)
                if c % 2 == 1:
                    i.then_inc(hidden_placed, 1)

        def expert_out(pe, n, e, k):
            pe.wait_ge(hidden_ready, 2 * n + 2)
            pe.wait_ge(y_used, n + (UNROLL - 1))
            for s in range(ST):
                for c in range(FC):
                    i = nc.tensor.matmul(psum[:, 6 + k % 2, s * D:(s + 1) * D], hidden[:, k % 2, c, s * P:(s + 1) * P],
                                         w2_sb[:, e, c, :], start=c == 0, stop=c == FC - 1)
                    if s == 0 and c == 0:
                        i.then_inc(w1_used, 1)
            i.then_inc(y_placed, 1)

        def keep_slots_turned(act, n, k):
            act.wait_ge(slot_xn_t_placed, n + 1)
            nc.scalar.copy(slot_xn_t[:, k % 2, :], psum[:, k % 2, 0:CAP]).then_inc(slot_xn_t_ready, 1)

        def rectify(act, n, k):
            for c in range(0, FC, 2):
                act.wait_ge(hidden_placed, 2 * n + c // 2 + 1)
                nc.scalar.activation(hidden[:, k % 2, c:c + 2, :],
                                     psum[:, 2 + 2 * (k % 2) + c // 2, :].rearrange("p (c n) -> p c n", c=2),
                                     ACT.Relu).then_inc(hidden_ready, 1)

        def scatter_rows(pool, n, k, layer):
            pool.wait_ge(y_used, n + (UNROLL + 1))
            pass_wait(pool)
            for s in range(ST):
                pool.indirect_dma_start(
                    out=rows_of[layer][:, :],
                    out_offset=bass.IndirectOffsetOnAxis(ap=new_rows[:, k, s, D:D + 1].bitcast(U32), axis=0),
                    in_=new_rows[:, k, s, 0:D], in_offset=None, bounds_check=TOKENS - 1,
                    oob_is_err=False).then_inc(rows_written[k], 16)

        def pool_experts(pool, layer):
            def body(i, last):
                for k in range(UNROLL):
                    n = i * UNROLL + (layer * EXPERTS + k)
                    if not (last and k + 3 >= UNROLL):
                        invert_slot_deviation(pool, n + 3, (k + 3) % UNROLL)
                    scatter_rows(pool, n, k, layer)
            n = layer * EXPERTS
            for k in range(3):
                invert_slot_deviation(pool, n + k, k)
            with pool.Fori(0, EXPERTS // UNROLL - 1) as i:
                body(i, False)
            body(EXPERTS // UNROLL - 1, True)

        def pe_experts(pe, layer):
            def body(i, last):
                for k in range(UNROLL):
                    e = i * UNROLL + k
                    n = i * UNROLL + (layer * EXPERTS + k)
                    turn = i + layer * (EXPERTS // UNROLL)
                    if not (last and k + 1 >= UNROLL):
                        expert_in(pe, n + 1, turn + (k + 1) // UNROLL, (k + 1) % UNROLL)
                    if not (last and k + 2 >= UNROLL):
                        turn_slots(pe, n + 2, (k + 2) % UNROLL)
                    expert_out(pe, n, e, k)
            n = layer * EXPERTS
            turn_slots(pe, n, 0)
            turn_slots(pe, n + 1, 1)
            expert_in(pe, n, layer * (EXPERTS // UNROLL), 0)
            with pe.Fori(0, EXPERTS // UNROLL - 1) as i:
                body(i, False)
            body(EXPERTS // UNROLL - 1, True)

        def act_experts(act, layer):
            def body(i, last):
                for k in range(UNROLL):
                    n = i * UNROLL + (layer * EXPERTS + k)
                    if not (last and k + 1 >= UNROLL):
                        rectify(act, n + 1, (k + 1) % UNROLL)
                    if not (last and k + 2 >= UNROLL):
                        keep_slots_turned(act, n + 2, (k + 2) % UNROLL)
            n = layer * EXPERTS
            keep_slots_turned(act, n, 0)
            keep_slots_turned(act, n + 1, 1)
            rectify(act, n, 0)
            with act.Fori(0, EXPERTS // UNROLL - 1) as i:
                body(i, False)
            body(EXPERTS // UNROLL - 1, True)

        def dve_experts(dve, layer):
            def body(i, last):
                for k in range(UNROLL):
                    n = i * UNROLL + (layer * EXPERTS + k)
                    turn = i + layer * (EXPERTS // UNROLL)
                    if not (last and k + 2 >= UNROLL):
                        dve.wait_ge(slot_xn_t_placed, n + 1)
                        normalize_slots(dve, n + 2, (k + 2) % UNROLL)
                    if not (last and k + 3 >= UNROLL):
                        measure_slots(dve, n + 3, turn + (k + 3) // UNROLL, (k + 3) % UNROLL)
                    add_expert(dve, n, turn, k)
            n, turn = layer * EXPERTS, layer * (EXPERTS // UNROLL)
            for k in range(2):
                measure_slots(dve, n + k, turn, k)
            for k in range(2):
                normalize_slots(dve, n + k, k)
            measure_slots(dve, n + 2, turn, 2)
            with dve.Fori(0, EXPERTS // UNROLL - 1) as i:
                body(i, False)
            body(EXPERTS // UNROLL - 1, True)


        OUT_T, MISC, RING, MAXIMA = 0, 1, 2, 4

        class Place:

            def __init__(self, base, at):
                self.bank = RING + at % 2
                self.free = base + (at + 1)
                self.placed = base + (at + 1)
                self.kept = base + (at + 3)

        def batch_places(prep, follows):
            beside = {(g, 1): ("shift", g) for g in range(QUADS) if g < 3 or follows}
            if prep:
                beside |= {(1, 4): "turn", (1, 9): ("project", 0), (1, 12): ("project", 1), (2, 4): ("project", 2),
                           (2, 9): ("project", 3), (2, 12): "v"}
            order = []
            for g in range(QUADS):
                for u in range(16):
                    order.append((g, u))
                    if (g, u) in beside:
                        order.append(beside[g, u])
            return order

        PREPARED = ("turn", ("project", 0), ("project", 1), ("project", 2), ("project", 3), "v")
        FIRST_SHIFT = Place(2 * len(PREPARED), 0)
        WHOLE_BATCH = len(batch_places(True, True))
        assert WHOLE_BATCH % 2 == 0 and len(PREPARED) % 2 == 0

        def prologue_place(n, what):
            return Place(n * len(PREPARED), PREPARED.index(what))

        def ring_base(b):
            base = b * WHOLE_BATCH + 2 * len(PREPARED)
            return base - len(PREPARED) if isinstance(b, int) and b == BATCH - 1 else base

        def batch_place(b, prep, follows, what):
            return Place(ring_base(b), 1 + batch_places(prep, follows).index(what))

        def before_batch(b):
            return ring_base(b) + 1

        def load_prep(sp, n):
            sp.wait_ge(prep_xn_ready, n)
            sp.dma_start(prep_x[:, :, :], x1[bass.ds(n * SEQ, SEQ), :].rearrange("(t p) d -> p t d", p=P)
                         ).then_inc(prep_x_loaded, 16)

        def prep_measure(dve, n):
            dve.wait_ge(prep_x_loaded, (n + 1) * 16)
            for t in range(TT):
                i = nc.vector.bn_stats(prep_stats[:, t, :], prep_x[:, t, :])
            i.then_inc(prep_stats_ready, 1)
            dve.wait_ge(prep_stats_ready, n * 2 + 1)
            pass_wait(dve)
            for t in range(TT):
                i = nc.vector.bn_aggr(prep_moments[:, t, :], prep_stats[:, t, :])
            i.then_inc(prep_stats_ready, 1)
            dve.wait_ge(prep_stats_ready, n * 2 + 2)
            nc.vector.tensor_scalar(prep_spread[:, :], prep_moments[:, :, 1], EPS, None, ALU.add
                                    ).then_inc(prep_moments_ready, 1)

        def prep_normalize(pool, n, turned_before):
            pool.wait_ge(prep_moments_ready, n + 1)
            nc.gpsimd.tensor_tensor(prep_rstd[:, :], prep_spread[:, :], minus_half[:, :], ALU.pow
                                    ).then_inc(prep_rstd_ready, 1)
            pool.wait_ge(prep_rstd_ready, n + 1)
            pool.wait_ge(ring_placed, turned_before)
            pass_wait(pool)
            for t in range(TT):
                i = nc.gpsimd.tensor_scalar(prep_xn[:, t, :], prep_x[:, t, :], prep_moments[:, t, 0:1],
                                            prep_rstd[:, t:t + 1], ALU.subtract, ALU.mult)
            i.then_inc(prep_xn_ready, 1)

        def prep_turn(pe, n, place):
            pe.wait_ge(prep_xn_ready, n + 1)
            pe.wait_ge(ring_used, place.free)
            for t in range(TT):
                i = nc.tensor.transpose(psum[:, place.bank, t * P:(t + 1) * P], prep_xn[:, t, :], ident[:, :])
            i.then_inc(ring_placed, 1)

        def prep_keep_turned(act, place):
            act.wait_ge(ring_placed, place.placed)
            nc.scalar.copy(prep_xn_t[:, :], psum[:, place.bank, :]).then_inc(ring_used, 1)

        def project(pe, c, turn, place):
            pe.wait_ge(ring_used, turn.kept)
            pe.wait_ge(ring_used, place.free)
            w = (wq_sb, wk_sb)[c // 2][:, c % 2, :]
            nc.tensor.matmul(psum[:, place.bank, :], w, prep_xn_t[:, :], start=True, stop=True).then_inc(ring_placed, 1)

        def keep_projection(act, n, c, place):
            act.wait_ge(ring_placed, place.placed)
            act.wait_ge(roped, n * 2 + (1 + c // 2))
            nc.scalar.activation(proj[:, c, :], psum[:, place.bank, :], ACT.Identity, bias=bias_sb[:, c:c + 1]
                                 ).then_inc(ring_used, 1)

        def project_v(pe, turn, place):
            pe.wait_ge(ring_used, turn.kept)
            pe.wait_ge(ring_used, place.free)
            for t in range(TT):
                i = nc.tensor.matmul(psum[:, place.bank, t * D:(t + 1) * D], prep_xn_t[:, t * P:(t + 1) * P],
                                     wv_sb[:, :], start=True, stop=True)
            i.then_inc(ring_placed, 1)

        def keep_v(act, n, place):
            act.wait_ge(ring_placed, place.placed)
            nc.scalar.copy(v_flat[:, bass.ds(n, 1), :, :].squeeze(1),
                           psum[:, place.bank, :].rearrange("p (t d) -> p t d", t=TT)).then_inc(ring_used, 1)

        def rotate(pool, n, c, place):
            pool.wait_ge(ring_used, place.kept)
            nc.gpsimd.tensor_tensor(proj[:, 2 * c, :], proj[:, 2 * c, :], rope_sb[:, 0, :], ALU.mult)
            nc.gpsimd.tensor_tensor(proj[:, 2 * c + 1, :], proj[:, 2 * c + 1, :], rope_sb[:, 1, :], ALU.mult
                                    ).then_inc(rope_step, 1)
            pool.wait_ge(rope_step, n * 2 + (c + 1))
            nc.gpsimd.tensor_tensor(turned[:, c, :], proj[:, 2 * c, :], proj[:, 2 * c + 1, :], ALU.add
                                    ).then_inc(roped, 1)

        def keep_first_part(act, n, c):
            act.wait_ge(roped, n * 2 + (c + 3))
            act.wait_ge(parts_written[c], n * (16 * len(PART_SLOTS[c])))
            nc.scalar.copy(parts[:, c, 0, :], turned[:, c, :]).then_inc(first_part_ready, 1)

        def take_rest(pool, n, c):
            pool.wait_ge(first_part_ready, n * 2 + (c + 1))
            nc.gpsimd.tensor_tensor(turned[:, c, :], turned[:, c, :], parts[:, c, 0, :], ALU.subtract
                                    ).then_inc(rest_ready, 1)

        def keep_second_part(act, n, c):
            act.wait_ge(rest_ready, n * 2 + (c + 1))
            nc.scalar.copy(parts[:, c, 1, :], turned[:, c, :]).then_inc(second_part_ready, 1)

        def keep_third_part(pool, n, c):
            pool.wait_ge(second_part_ready, n * 2 + (c + 1))
            nc.gpsimd.tensor_tensor(parts[:, c, 2, :], turned[:, c, :], parts[:, c, 1, :], ALU.subtract
                                    ).then_inc(parts_ready, 1)

        def write_parts(sp, n, c):
            sp.wait_ge(parts_ready, n * 2 + (c + 1))
            for first, last, step, part in PART_SLOTS[c]:
                count = (last - first) // step + 1
                sp.dma_start(qk_rows[bass.ds(n, 1), c, first:last + 1:step, :, :].squeeze(0)
                             .rearrange("s f t -> f s t"),
                             parts[:, c, part, :].unsqueeze(1).broadcast_to([P, count, SEQ])
                             ).then_inc(parts_written[c], 16)

        def load_quad(sp, n, g):
            for c in range(2):
                sp.wait_ge(parts_written[c], (n + 1) * (16 * len(PART_SLOTS[c])))
                pass_wait(sp)
            for c in range(2):
                for h in range(2):
                    ring = (q_ring[:, g, h, :, :], k_ring[:, g, :, :])[c]
                    features = slice(16 * (2 * g + h), 16 * (2 * g + h + 1))
                    src = qk_rows[bass.ds(n, 1), c, :, features, :].squeeze(0)
                    sp.dma_start(ring[64 * h:64 * h + ROWS, :, :].rearrange("p h s -> p (h s)"),
                                 src.rearrange("s (d h) t -> s d (h t)", h=2)).then_inc(quad_loaded[g], 16)

        def fill_v(pool, n, g, kept):
            pool.wait_ge(ring_used, kept)
            flat = v_flat[:, bass.ds(n, 1), :, :].squeeze(1)
            nc.gpsimd.tensor_tensor(
                v_ring[:, g, :, :, 0:HEAD_DIM],
                flat[:, :, 32 * g:32 * g + 32].rearrange("p t (h d) -> p t h d", h=4),
                v_bias_sb[:, 32 * g:32 * g + 32].rearrange("p (h d) -> p h d", h=4).unsqueeze(1)
                .broadcast_to([P, TT, 4, HEAD_DIM]), ALU.add).then_inc(v_filled, 1)

        def max_tile(pe, q, g, w):
            h, tile = divmod(w // 2, TT)
            if w % 2 == 0:
                pe.wait_ge(max_used, q * 8 + (w // 2 + 1))
            i = nc.tensor.matmul(psum[:, MAXIMA + w % 4, :], q_ring[0:SHIFT_ROW, g, w % 2, h, tile * P:(tile + 1) * P],
                                 k_ring[0:SHIFT_ROW, g, h, :], start=True, stop=True)
            if w % 2 == 1:
                i.then_inc(max_placed, 1)

        def take_max(dve, q, g, pair):
            bank = MAXIMA + 2 * (pair % 2)
            dve.wait_ge(max_placed, q * 8 + (pair + 1))
            nc.vector.tensor_reduce(neg_max[:, g % 2, pair::TT * 2], psum[:, bank:bank + 2, :], AX.X, ALU.max,
                                    negate=True).then_inc(max_used, 1)

        def turn_shift(pe, q, g, place):
            pe.wait_ge(max_used, q * 8 + 10)
            pe.wait_ge(ring_used, place.free)
            nc.tensor.transpose(psum[0:16, place.bank, 0:P], neg_max[:, g % 2, :], ident[:, :]).then_inc(ring_placed, 1)

        def keep_shift(act, q, place):
            act.wait_ge(ring_placed, place.placed)
            act.wait_ge(shift_loaded, q * SHIFT_DMAS * 16)
            nc.scalar.copy(shift[:, :], psum[0:16, place.bank, 0:P])
            nc.scalar.copy(shift_parts[:, 0, :], psum[0:16, place.bank, 0:P]).then_inc(ring_used, 1)

        def split_shift(pool, q, place):
            pool.wait_ge(ring_used, place.kept)
            nc.gpsimd.tensor_tensor(shift_rest[:, :], shift[:, :], shift_parts[:, 0, :], ALU.subtract
                                    ).then_inc(shift_step, 1)
            pool.wait_ge(shift_step, q * 2 + 1)
            pass_wait(pool)
            nc.gpsimd.tensor_copy(shift_parts[:, 1, :], shift_rest[:, :]).then_inc(shift_step, 1)
            pool.wait_ge(shift_step, q * 2 + 2)
            nc.gpsimd.tensor_tensor(shift_parts[:, 2, :], shift_rest[:, :], shift_parts[:, 1, :], ALU.subtract
                                    ).then_inc(shift_ready, 1)

        def load_shift(sp, q, g):
            sp.wait_ge(shift_ready, q + 1)
            for part in range(3):
                row = SHIFT_ROW + part
                sp.dma_start(q_ring[row:row + 1, g, :, :, :].rearrange("p r h (t c) -> p (r h t) c", c=P),
                             shift_parts[:, part, :]).then_inc(shift_loaded, 16)

        def score_tile(pe, q, g, u, place):
            tile, head = divmod(u, 4)
            h = head // 2
            if u == 0:
                pe.wait_ge(shift_loaded, (q + 1) * SHIFT_DMAS * 16)
            pe.wait_ge(ring_used, place.free)
            nc.tensor.matmul(psum[:, place.bank, :], k_ring[:, g, h, tile * P:(tile + 1) * P],
                             q_ring[:, g, head % 2, h, :], start=True, stop=True).then_inc(ring_placed, 1)

        def exponential(act, u, place):
            act.wait_ge(ring_placed, place.placed)
            nc.scalar.activation(probs[:, u // 4, u % 4, :], psum[:, place.bank, :], ACT.Exp, scale=SCALE
                                 ).then_inc(ring_used, 1)

        def weigh(pe, q, g, tile):
            if tile == 0:
                pe.wait_ge(v_filled, q + 1)
                pe.wait_ge(o_kept, q)
            for head in range(4):
                i = nc.tensor.matmul(psum[32 * head:32 * head + 32, OUT_T, :], v_ring[:, g, tile, head, :],
                                     probs[:, tile, head, :], start=tile == 0, stop=tile == TT - 1,
                                     skip_group_check=True)
            if tile == TT - 1:
                i.then_inc(o_placed, 1)

        def keep_sums(act, q):
            act.wait_ge(o_placed, q + 1)
            nc.scalar.copy(out_t[:, :], psum[:, OUT_T, :]).then_inc(o_kept, 1)

        def turn_sums(pe, q):
            pe.wait_ge(o_kept, q + 1)
            for t in range(TT):
                i = nc.tensor.transpose(psum[:, MISC, t * P:(t + 1) * P], out_t[:, t * P:(t + 1) * P], ident[:, :])
            i.then_inc(o_turned, 1)

        def divide(dve, q, g):
            sums = psum[:, MISC, :].rearrange("p (t h c) -> p t h c", t=TT, h=4)
            dve.wait_ge(o_turned, q + 1)
            nc.vector.reciprocal(weight[:, :, :], sums[:, :, :, HEAD_DIM]).then_inc(weight_ready, 1)
            dve.wait_ge(weight_ready, q + 1)
            nc.vector.tensor_tensor(
                attended[:, :, 32 * g:32 * g + 32].rearrange("p t (h d) -> p t h d", h=4), sums[:, :, :, 0:HEAD_DIM],
                weight[:, :, :].unsqueeze(3).broadcast_to([P, TT, 4, HEAD_DIM]), ALU.mult).then_inc(attended_ready, 1)

        def load_residual(sp, b):
            sp.wait_ge(x2_ready, b)
            sp.dma_start(residual[:, :, :], x1[bass.ds(b * SEQ, SEQ), :].rearrange("(t p) d -> p t d", p=P)
                         ).then_inc(residual_loaded, 16)

        def add_residual(dve, b):
            dve.wait_ge(residual_loaded, (b + 1) * 16)
            dve.wait_ge(attended_ready, b * 4 + 5)
            dve.wait_ge(dispatched[0], b * (16 * TT) + 16 * TT * BATCH // 2)
            dve.wait_ge(x2_passed, b * 16 + 16)
            nc.vector.tensor_tensor(stage[:, 0, :, 0:D], residual[:, :, :], attended[:, :, :], ALU.add
                                    ).then_inc(x2_ready, 1)
            dve.wait_ge(x2_ready, b + 1)

        def pass_x2(sp, b):
            sp.wait_ge(x2_ready, b + 1)
            sp.dma_start(out[bass.ds(b * SEQ, SEQ), :].rearrange("(t p) d -> p t d", p=P), stage[:, 0, :, 0:D]
                         ).then_inc(x2_passed, 16)

        def pe_batch(pe, b, below, prep, follows):
            def place(*what):
                return batch_place(b, prep, follows, what if len(what) > 1 else what[0])
            for g in range(QUADS):
                q = b * 4 + g
                for u in range(16):
                    score_tile(pe, q, g, u, place(g, u))
                    if u % 4 < 2 and (g < 2 or follows):
                        if u == 0:
                            pe.wait_ge(quad_loaded[(g + 2) % 4], (b + (1 + (g + 2) // 4)) * 64)
                        for w in range(2):
                            max_tile(pe, q + 2, (g + 2) % 4, u // 4 * 4 + u % 4 * 2 + w)
                    if u == 1 and (g < 3 or follows):
                        turn_shift(pe, q + 1, (g + 1) % 4, place("shift", g))
                    if u % 4 == 3:
                        tile = (u // 4 + 3) % 4
                        if tile < 3:
                            weigh(pe, q, g, tile)
                        elif g > 0:
                            weigh(pe, q - 1, g - 1, tile)
                        elif below is not None:
                            weigh(pe, below * 4 + 3, 3, tile)
                    if u == 8:
                        if g == 2:
                            pe.wait_ge(below_ready, b + BATCH)
                        if g == 3:
                            pe.wait_ge(route_ready, b + BATCH)
                        if g > 0:
                            turn_sums(pe, q - 1)
                        elif below is not None:
                            turn_sums(pe, below * 4 + 3)
                    if prep:
                        if (g, u) == (1, 4):
                            prep_turn(pe, b + 2, place("turn"))
                        if (g, u) == (1, 9):
                            project(pe, 0, place("turn"), place("project", 0))
                        if (g, u) == (1, 12):
                            project(pe, 1, place("turn"), place("project", 1))
                        if (g, u) == (2, 4):
                            project(pe, 2, place("turn"), place("project", 2))
                        if (g, u) == (2, 9):
                            project(pe, 3, place("turn"), place("project", 3))
                        if (g, u) == (2, 12):
                            project_v(pe, place("turn"), place("v"))
                    if below is not None:
                        if (g, u) == (1, 13):
                            pe.wait_ge(attended_ready, q + 1)
                            turn_tokens(pe, below + BATCH, 0, MISC)
                        if (g, u) == (2, 0):
                            gate_logits(pe, below + BATCH, 0, MISC)
                        if (g, u) == (2, 13):
                            pe.wait_ge(attended_ready, q + 1)
                            count_places(pe, below + BATCH, MISC)

        def act_batch(act, b, below, prep, follows):
            def place(*what):
                return batch_place(b, prep, follows, what if len(what) > 1 else what[0])
            for g in range(QUADS):
                q = b * 4 + g
                for u in range(16):
                    exponential(act, u, place(g, u))
                    if u == 1 and (g < 3 or follows):
                        keep_shift(act, q + 1, place("shift", g))
                    if u == 5:
                        if g > 0:
                            keep_sums(act, q - 1)
                        elif below is not None:
                            keep_sums(act, below * 4 + 3)
                    if prep:
                        if (g, u) == (1, 4):
                            prep_keep_turned(act, place("turn"))
                        if (g, u) == (1, 9):
                            keep_projection(act, b + 2, 0, place("project", 0))
                        if (g, u) == (1, 12):
                            keep_projection(act, b + 2, 1, place("project", 1))
                        if (g, u) == (2, 4):
                            keep_projection(act, b + 2, 2, place("project", 2))
                        if (g, u) == (2, 9):
                            keep_projection(act, b + 2, 3, place("project", 3))
                        if (g, u) == (2, 12):
                            keep_v(act, b + 2, place("v"))
                        if (g, u) == (2, 14):
                            keep_first_part(act, b + 2, 0)
                        if (g, u) == (3, 1):
                            keep_first_part(act, b + 2, 1)
                        if (g, u) == (3, 9):
                            keep_second_part(act, b + 2, 0)
                        if (g, u) == (3, 12):
                            keep_second_part(act, b + 2, 1)
                    if below is not None:
                        if (g, u) == (1, 14):
                            keep_turned(act, below + BATCH, 0, MISC)
                        if (g, u) == (2, 3):
                            gate_exponentials(act, below + BATCH)

        def dve_batch(dve, b, below, prep, follows):
            r = None if below is None else below + BATCH
            for g in range(QUADS):
                q = b * 4 + g
                for pair in range(8):
                    if g < 2 or follows:
                        take_max(dve, q + 2, (g + 2) % 4, pair)
                    if (g, pair) == (0, 2) and prep:
                        prep_measure(dve, b + 2)
                    if pair == 4:
                        if g > 0:
                            divide(dve, q - 1, g - 1)
                        elif below is not None:
                            divide(dve, below * 4 + 3, 3)
                            add_residual(dve, below)
                    if (g, pair) == (0, 5) and below is not None:
                        measure(dve, Steps(dve, route_step, route_start(r)), 0)
                    if (g, pair) == (1, 1) and below is not None:
                        normalize(dve, r, 0)
                    if (g, pair) == (2, 1) and below is not None:
                        choose(dve, Steps(dve, route_step, route_start(r) + 2), r, MISC)
                    if (g, pair) == (2, 7) and below is not None:
                        route(dve, Steps(dve, route_step, route_start(r) + 7), r, 0, MISC, below)

        def pool_batch(pool, b, below, prep, follows):
            r = None if below is None else below + BATCH
            v_kept = before_batch(b) + 2
            def place(*what):
                return batch_place(b, prep, follows, what)
            for g in range(QUADS):
                q = b * 4 + g
                if g < 3 or follows:
                    split_shift(pool, q + 1, place("shift", g))
                if g == 0 and below is not None:
                    pool.wait_ge(o_placed, q)
                    fill_v(pool, b, 3, v_kept)
                if g > 0 and follows:
                    pool.wait_ge(o_placed, q)
                    fill_v(pool, b + 1, g - 1, v_kept)
                if g == 0:
                    if prep:
                        prep_normalize(pool, b + 2, before_batch(b))
                    if below is not None:
                        invert_deviation(pool, r)
                if g == 2 and prep:
                    rotate(pool, b + 2, 0, place("project", 1))
                    rotate(pool, b + 2, 1, place("project", 3))
                if g == 3:
                    if prep:
                        take_rest(pool, b + 2, 0)
                        take_rest(pool, b + 2, 1)
                        keep_third_part(pool, b + 2, 0)
                        keep_third_part(pool, b + 2, 1)
                    if below is not None:
                        scatter_tokens(pool, r, 0, 1)

        def sp_batch(sp, b, below, prep, follows):
            for g in range(QUADS):
                q = b * 4 + g
                if g == 0 and prep:
                    load_prep(sp, b + 2)
                if g == 0 or follows:
                    sp.wait_ge(ring_placed, before_batch(b) if g == 0 else
                               batch_place(b, prep, follows, (g - 1, 15)).placed)
                    pass_wait(sp)
                    load_quad(sp, b + (g > 0), (g + 3) % 4)
                if g < 3 or follows:
                    load_shift(sp, q + 1, (g + 1) % 4)
                if g == 0 and below is not None:
                    pass_x2(sp, below)
                    if follows:
                        for c in range(2):
                            write_parts(sp, b + 1, c)
                if g == 1:
                    load_residual(sp, b)

        def route_all(eng, body):
            with eng.Fori(0, BATCH // 2 - 1) as i:
                for s in range(2):
                    body(i * 2 + s, i, s, False)
            for s in range(2):
                body(BATCH - 2 + s, BATCH // 2 - 1, s, s == 1)

        def route_start(r):
            return r * ROUTE_STEPS + 2

        def attend_all(eng, body):
            body(eng, 0, None, True, True)
            with eng.Fori(0, BATCH - 3) as below:
                body(eng, below + 1, below, True, True)
            body(eng, BATCH - 2, BATCH - 3, False, True)
            body(eng, BATCH - 1, BATCH - 2, False, False)

        LAST_QUAD = BATCH * QUADS - 1
        LAST_ROUTED = 2 * BATCH - 1

        @block.sync
        def _(sp):
            loads = [(ident[:, :], identity), (counters[:, :, :], count_mats), (iota_e[:, :], expert_iota[0]),
                     (iota_low[:, :], expert_iota[1]), (numbers[:, :], token_number), (wg_sb[:, :], wg),
                     (wq_sb[:, :, :], wq_t), (wk_sb[:, :, :], wk_t), (wv_sb[:, :], wv_t), (bias_sb[:, :], qk_bias),
                     (v_bias_sb[:, :], v_bias.broadcast_to([P, D])), (rope_sb[:, :, :], rope)]
            assert len(loads) == CONSTS
            for dst, src in loads:
                sp.dma_start(dst, src).then_inc(consts_loaded, 16)
            sp.wait_ge(empty_ready, 3)
            for k in range(2):
                sp.dma_start(slots[k].rearrange("(n p) c -> p n c", p=P),
                             empty[:, :].unsqueeze(1).broadcast_to([P, TOKENS // P, ROW])).then_inc(slots_cleared, 16)
            with sp.Fori(0, BATCH // 2) as i:
                for s in range(2):
                    b = i * 2 + s
                    sp.wait_ge(dispatched[s], i * (16 * TT))
                    sp.dma_start(stage[:, s, :, 0:D], x[bass.ds(b * SEQ, SEQ), :].rearrange("(t p) d -> p t d", p=P)
                                 ).then_inc(x_loaded[s], 16)
            sp.dma_start(x1, x).then_inc(x_passed, 16)
            for e in range(0, EXPERTS, 4):
                sp.dma_start(w2_sb[:, e:e + 4, :, :], w2[e:e + 4].rearrange("e (c p) d -> p e c d", p=P)
                             ).then_inc(w2_loaded, 16)
            for k in range(UNROLL):
                load_w1(sp, 0, 0, k)
            load_experts(sp, 0)
            for k in range(UNROLL):
                load_w1(sp, 1, 0, k)
            for k in range(UNROLL):
                sp.wait_ge(rows_written[k], 16 * ST * (EXPERTS // UNROLL))
            with sp.Fori(0, 2) as n:
                load_prep(sp, n)
                for c in range(2):
                    write_parts(sp, n, c)
            for g in range(3):
                load_quad(sp, 0, g)
            load_shift(sp, 0, 0)
            attend_all(sp, sp_batch)
            pass_x2(sp, BATCH - 1)
            load_experts(sp, 1)
            for k in range(UNROLL):
                sp.wait_ge(rows_written[k], 2 * 16 * ST * (EXPERTS // UNROLL))

        @block.gpsimd
        def _(pool):
            nc.gpsimd.memset(minus_half[:, :], -0.5).then_inc(empty_ready, 1)
            nc.gpsimd.memset(empty[:, :], 0.0).then_inc(empty_ready, 1)
            pool.wait_ge(empty_ready, 2)
            nc.gpsimd.memset(empty[:, D:D + 1].bitcast(I32), NOWHERE).then_inc(empty_ready, 1)
            nc.gpsimd.memset(k_ring[:, :, :, :], 1.0)
            nc.gpsimd.memset(q_ring[:, :, :, :, :], 0.0)
            nc.gpsimd.memset(v_ring[:, :, :, :, :], 0.0).then_inc(ring_cleared, 1)
            pool.wait_ge(ring_cleared, 1)
            nc.gpsimd.memset(v_ring[:, :, :, :, HEAD_DIM:HEAD_DIM + 1], 1.0).then_inc(ring_cleared, 1)
            pool.wait_ge(ring_cleared, 2)
            pool.wait_ge(slots_cleared, 32)

            def body(b, i, s, last):
                if not last:
                    invert_deviation(pool, b + 1)
                scatter_tokens(pool, b, s, 0)
            invert_deviation(pool, 0)
            route_all(pool, body)
            pool.wait_ge(x_passed, 16)
            pool_experts(pool, 0)
            with pool.Fori(0, 2) as n:
                prep_normalize(pool, n, n * len(PREPARED))
                for c in range(2):
                    rotate(pool, n, c, prologue_place(n, ("project", 2 * c + 1)))
                    take_rest(pool, n, c)
                    keep_third_part(pool, n, c)
            for g in range(QUADS):
                fill_v(pool, 0, g, prologue_place(0, "v").kept)
            split_shift(pool, 0, FIRST_SHIFT)
            attend_all(pool, pool_batch)
            invert_deviation(pool, LAST_ROUTED)
            scatter_tokens(pool, LAST_ROUTED, 0, 1)
            pool.wait_ge(x2_passed, 16 + 16 * BATCH)
            pool_experts(pool, 1)

        @block.vector
        def _(dve):
            nc.vector.memset(carry[:, :], 0.0).then_inc(route_step, 1)
            dve.wait_ge(consts_loaded, 16 * CONSTS)

            def measure_staged(steps, i, s):
                dve.wait_ge(x_loaded[s], (i + 1) * 16)
                measure(dve, steps, s)

            def body(b, i, s, last):
                steps = Steps(dve, route_step, b * ROUTE_STEPS + 3)
                if not last:
                    measure_staged(steps, i + s, 1 - s)
                choose(dve, steps, b, 2 + s)
                if not last:
                    normalize(dve, b + 1, 1 - s)
                route(dve, steps, b, s, 2 + s, b)
                assert last or steps.n == ROUTE_STEPS
            measure_staged(Steps(dve, route_step, 1), 0, 0)
            normalize(dve, 0, 0)
            route_all(dve, body)
            nc.vector.memset(carry[:, :], 0.0).then_inc(route_step, 1)
            dve_experts(dve, 0)
            with dve.Fori(0, 2) as n:
                prep_measure(dve, n)
            for g in range(2):
                for pair in range(8):
                    take_max(dve, g, g, pair)
            attend_all(dve, dve_batch)
            divide(dve, LAST_QUAD, QUADS - 1)
            add_residual(dve, BATCH - 1)
            steps = Steps(dve, route_step, route_start(LAST_ROUTED))
            measure(dve, steps, 0)
            normalize(dve, LAST_ROUTED, 0)
            choose(dve, steps, LAST_ROUTED, MISC)
            route(dve, steps, LAST_ROUTED, 0, MISC, BATCH - 1)
            dve_experts(dve, 1)

        @block.scalar
        def _(act):
            act.sem_inc(y_used, UNROLL)
            act.sem_inc(w1_used, UNROLL)
            act.sem_inc(roped, 2)
            act.sem_inc(max_used, 2)
            act.sem_inc(ring_used, 2)
            act.sem_inc(attended_ready, 1)
            act.sem_inc(x2_passed, 16)
            act.wait_ge(consts_loaded, 16 * CONSTS)

            def body(b, i, s, last):
                gate_exponentials(act, b)
                if not last:
                    keep_turned(act, b + 1, 1 - s, 1 - s)
            keep_turned(act, 0, 0, 0)
            route_all(act, body)
            act_experts(act, 0)
            with act.Fori(0, 2) as n:
                prep_keep_turned(act, prologue_place(n, "turn"))
                for c in range(4):
                    keep_projection(act, n, c, prologue_place(n, ("project", c)))
                keep_v(act, n, prologue_place(n, "v"))
                for c in range(2):
                    keep_first_part(act, n, c)
                    keep_second_part(act, n, c)
            keep_shift(act, 0, FIRST_SHIFT)
            attend_all(act, act_batch)
            keep_sums(act, LAST_QUAD)
            keep_turned(act, LAST_ROUTED, 0, MISC)
            gate_exponentials(act, LAST_ROUTED)
            act_experts(act, 1)

        @block.tensor
        def _(pe):
            pe.wait_ge(consts_loaded, 16 * CONSTS)

            def body(b, i, s, last):
                gate_logits(pe, b, s, 2 + s)
                if not last:
                    turn_tokens(pe, b + 1, 1 - s, 1 - s)
                count_places(pe, b, 2 + s)
            turn_tokens(pe, 0, 0, 0)
            route_all(pe, body)
            pe.wait_ge(w2_loaded, 16 * 4)
            pe_experts(pe, 0)
            with pe.Fori(0, 2) as n:
                turn = prologue_place(n, "turn")
                prep_turn(pe, n, turn)
                for c in range(4):
                    project(pe, c, turn, prologue_place(n, ("project", c)))
                project_v(pe, turn, prologue_place(n, "v"))
            pe.wait_ge(ring_cleared, 2)
            for g in range(2):
                pe.wait_ge(quad_loaded[g], 64)
                for w in range(16):
                    max_tile(pe, g, g, w)
            turn_shift(pe, 0, 0, FIRST_SHIFT)
            attend_all(pe, pe_batch)
            pe.wait_ge(ring_used, batch_place(BATCH - 1, False, False, (QUADS - 1, 15)).kept)
            weigh(pe, LAST_QUAD, QUADS - 1, TT - 1)
            pe.wait_ge(attended_ready, LAST_QUAD + 1)
            turn_sums(pe, LAST_QUAD)
            pe.wait_ge(attended_ready, LAST_QUAD + 2)
            turn_tokens(pe, LAST_ROUTED, 0, MISC)
            gate_logits(pe, LAST_ROUTED, 0, MISC)
            count_places(pe, LAST_ROUTED, MISC)
            pe_experts(pe, 1)


def kernel(L0_attn_x, L0_attn_wq_w, L0_attn_wq_b, L0_attn_wk_w, L0_attn_wk_b, L0_attn_wv_w, L0_attn_wv_b,
           L0_ffn_Wg, L0_ffn_w1, L0_ffn_w2):
    import ml_dtypes
    import numpy as np
    import concourse.bacc as bacc
    from concourse.bass_utils import run_bass_kernel_spmd

    quad, par, feat, pair = np.meshgrid(np.arange(QUADS), np.arange(2), np.arange(HEAD_DIM), np.arange(2),
                                        indexing="ij")
    order = ((4 * quad + 2 * pair + par) * HEAD_DIM + feat).reshape(-1)
    partner = order ^ 1
    feature = feat.reshape(-1)

    theta = np.float32(10000.0) ** (np.float32(-2.0) * np.arange(HEAD_DIM // 2, dtype=np.float32)
                                    / np.float32(HEAD_DIM))
    angle = np.outer(np.arange(SEQ, dtype=np.float32), theta.astype(np.float32)).astype(np.float32)
    cosine = np.cos(angle).T[feature // 2]
    sine = np.sin(angle).T[feature // 2] * np.where(feature % 2 == 0, -1.0, 1.0)[:, None]

    a = np.asarray
    arrays = {
        "x": a(L0_attn_x).reshape(TOKENS, D),
        "wq_t": np.stack([a(L0_attn_wq_w)[order].T, a(L0_attn_wq_w)[partner].T], axis=1),
        "wk_t": np.stack([a(L0_attn_wk_w)[order].T, a(L0_attn_wk_w)[partner].T], axis=1),
        "wv_t": a(L0_attn_wv_w).T,
        "qk_bias": np.stack([a(L0_attn_wq_b)[order], a(L0_attn_wq_b)[partner],
                             a(L0_attn_wk_b)[order], a(L0_attn_wk_b)[partner]], axis=1),
        "v_bias": a(L0_attn_wv_b).reshape(1, D),
        "wg": a(L0_ffn_Wg),
        "w1": a(L0_ffn_w1),
        "w2": a(L0_ffn_w2),
        "rope": np.stack([cosine, sine], axis=1).astype(np.float32),
        "identity": np.eye(P, dtype=np.float32),
        "count_mats": np.stack([np.triu(np.ones((P, P)), 1), np.ones((P, P))], axis=1).astype(ml_dtypes.bfloat16),
        "expert_iota": np.stack([np.tile(np.arange(EXPERTS), (P, 1)), np.tile(np.arange(EXPERTS) - EXPERTS, (P, 1))]
                                ).astype(np.float32),
        "token_number": np.arange(TOKENS, dtype=np.int32).reshape(-1, P).T,
    }
    arrays = {name: np.ascontiguousarray(v) for name, v in arrays.items()}
    nc = bacc.Bacc("TRN2", target_bir_lowering=False, num_devices=1)
    args = [nc.dram_tensor(name, v.shape, mybir.dt.from_np(v.dtype), kind="ExternalInput").ap()
            for name, v in arrays.items()]
    out = nc.dram_tensor("out", (TOKENS, D), F32, kind="ExternalOutput").ap()
    macaron_block_kernel(nc, *args, out)
    r = run_bass_kernel_spmd(nc, [arrays], core_ids=[0])
    return r.results[0]["out"].reshape(BATCH, SEQ, D)
```

```python
from contextlib import ExitStack

import concourse.bass as bass
from concourse import mybir

ALU = mybir.AluOpType
ACT = mybir.ActivationFunctionType
AX = mybir.AxisListType
F32 = mybir.dt.float32
BF16 = mybir.dt.bfloat16
I32 = mybir.dt.int32
U32 = mybir.dt.uint32

P = 128
BATCH, SEQ, D = 8, 512, 128
TOKENS = BATCH * SEQ
TT = SEQ // P
EXPERTS, HID = 16, 512
CAP = TOKENS // EXPERTS
ST = CAP // P
FC = HID // P
ROW = D + 2
EPS = 1e-5
NOWHERE = 1 << 20
UNROLL = 4


class Steps:

    def __init__(self, eng, sem, start=0):
        self.eng, self.sem, self.start, self.n = eng, sem, start, 0

    def did(self, instruction):
        instruction.then_inc(self.sem, 1)
        self.n += 1

    def settle(self):
        self.eng.wait_ge(self.sem, self.start + self.n)


ROUTE_STEPS = 16
STAGES = 4
HEADS, HEAD_DIM = 16, 8
QUADS = HEADS // 4
Q_PARTS = (0, 0, 0, 1, 1, 2)
K_PARTS = (0, 1, 2, 0, 1, 0)
SLOTS = len(Q_PARTS)
PART_SLOTS = (((0, 2, 1, 0), (3, 4, 1, 1), (5, 5, 1, 2)),
              ((0, 3, 3, 0), (5, 5, 1, 0), (1, 4, 3, 1), (2, 2, 1, 2)))
ROWS = SLOTS * HEAD_DIM
SHIFT_ROW = 64 + ROWS
SHIFT_DMAS = 3


def macaron_block_kernel(nc, x, wq_t, wk_t, wv_t, qk_bias, v_bias, wg, w1, w2, rope, identity, count_mats,
                         expert_iota, token_number, out):
    SCALE = 1.0 / float(HEAD_DIM) ** 0.5

    with ExitStack() as ctx:
        def sb(name, shape, dt):
            return ctx.enter_context(nc.sbuf_tensor(name, shape, dt))

        def sem(name):
            return ctx.enter_context(nc.semaphore(name))

        x1 = nc.dram_tensor("x1", (TOKENS, D), F32).ap()
        slots = [nc.dram_tensor(f"slots{k}", (TOKENS, ROW), F32).ap() for k in range(2)]
        rows_of = [x1, out]

        ident = sb("ident", [P, P], F32)
        counters = sb("counters", [P, 2, P], BF16)
        iota_e = sb("iota_e", [P, EXPERTS], F32)
        iota_low = sb("iota_low", [P, EXPERTS], F32)
        numbers = sb("numbers", [P, TOKENS // P], I32)
        wg_sb = sb("wg_sb", [P, EXPERTS], F32)
        w2_sb = sb("w2_sb", [P, EXPERTS, FC, D], F32)
        w1_ring = sb("w1_ring", [P, UNROLL, HID], F32)
        empty = sb("empty", [P, ROW], F32)

        stage = sb("stage", [P, STAGES, TT, ROW], F32)
        xn = sb("xn", [P, 2, TT, D], F32)
        xn_t = sb("xn_t", [P, 2, SEQ], F32)
        stats = sb("stats", [P, TT, 6], F32)
        moments = sb("moments", [P, 2, TT, 2], F32)
        minus_half = sb("minus_half", [P, TT], F32)
        spread = sb("spread", [P, 2, TT], F32)
        rstd = sb("rstd", [P, 2, TT], F32)
        top = sb("top", [P, TT], F32)
        below = sb("below", [P, TT, EXPERTS], F32)
        tied = sb("tied", [P, TT, EXPERTS], F32)
        first = sb("first", [P, TT], F32)
        onehot = sb("onehot", [P, TT, EXPERTS], BF16)
        gate_exp = sb("gate_exp", [P, TT, EXPERTS], F32)
        place = sb("place", [P, TT, EXPERTS], F32)
        carry = sb("carry", [P, EXPERTS], F32)
        loc = sb("loc", [P, TT], F32)
        base = sb("base", [P, TT], F32)
        over = sb("over", [P, TT], F32)
        half = sb("half", [P, TT], F32)
        gate_sum = sb("gate_sum", [P, TT], F32)
        dest = sb("dest", [P, STAGES, TT], I32)

        slot_rows = sb("slot_rows", [P, UNROLL, ST, ROW], F32)
        new_rows = sb("new_rows", [P, UNROLL, ST, ROW], F32)
        slot_stats = sb("slot_stats", [P, ST, 6], F32)
        slot_moments = sb("slot_moments", [P, 2, ST, 2], F32)
        slot_spread = sb("slot_spread", [P, 2, ST], F32)
        slot_rstd = sb("slot_rstd", [P, 2, ST], F32)
        slot_xn = sb("slot_xn", [P, 2, ST, D], F32)
        slot_xn_t = sb("slot_xn_t", [P, 2, CAP], F32)
        hidden = sb("hidden", [P, 2, FC, CAP], F32)

        psum = ctx.enter_context(nc.psum_tensor("psum", [P, 8, 512], F32))

        consts_loaded = sem("consts_loaded")
        weights_loaded = sem("weights_loaded")
        w2_loaded = sem("w2_loaded")
        x_passed = sem("x_passed")
        x_loaded = [sem(f"x_loaded{s}") for s in range(STAGES)]
        empty_ready = sem("empty_ready")
        waits_passed = sem("waits_passed")
        slots_cleared = [sem(f"slots_cleared{layer}") for layer in range(2)]
        w1_loaded = [sem(f"w1_loaded{k}") for k in range(UNROLL)]
        w1_used = sem("w1_used")
        slots_loaded = [sem(f"slots_loaded{k}") for k in range(UNROLL)]
        rows_written = [sem(f"rows_written{k}") for k in range(UNROLL)]
        dispatched = [sem(f"dispatched{s}") for s in range(STAGES)]
        xn_ready = sem("xn_ready")
        xn_t_placed = sem("xn_t_placed")
        xn_t_ready = sem("xn_t_ready")
        logits_ready = sem("logits_ready")
        below_ready = sem("below_ready")
        gate_exp_ready = sem("gate_exp_ready")
        onehot_ready = sem("onehot_ready")
        place_ready = sem("place_ready")
        route_ready = sem("route_ready")
        route_step = sem("route_step")
        moments_ready = sem("moments_ready")
        rstd_ready = sem("rstd_ready")
        slot_stats_ready = sem("slot_stats_ready")
        slot_moments_ready = sem("slot_moments_ready")
        slot_rstd_ready = sem("slot_rstd_ready")
        slot_xn_ready = sem("slot_xn_ready")
        slot_xn_t_placed = sem("slot_xn_t_placed")
        slot_xn_t_ready = sem("slot_xn_t_ready")
        hidden_placed = sem("hidden_placed")
        hidden_ready = sem("hidden_ready")
        y_placed = sem("y_placed")
        y_used = sem("y_used")

        wq_sb = sb("wq_sb", [P, 2, D], F32)
        wk_sb = sb("wk_sb", [P, 2, D], F32)
        wv_sb = sb("wv_sb", [P, D], F32)
        bias_sb = sb("bias_sb", [P, 4], F32)
        v_bias_sb = sb("v_bias_sb", [P, D], F32)
        rope_sb = sb("rope_sb", [P, 2, SEQ], F32)
        prep_x = sb("prep_x", [P, TT, D], F32)
        prep_stats = sb("prep_stats", [P, TT, 6], F32)
        prep_moments = sb("prep_moments", [P, TT, 2], F32)
        prep_spread = sb("prep_spread", [P, TT], F32)
        prep_rstd = sb("prep_rstd", [P, TT], F32)
        prep_xn = sb("prep_xn", [P, TT, D], F32)
        prep_xn_t = sb("prep_xn_t", [P, SEQ], F32)
        proj = sb("proj", [P, 4, SEQ], F32)
        turned = sb("turned", [P, 2, SEQ], F32)
        parts = sb("parts", [P, 2, 3, SEQ], BF16)
        v_flat = sb("v_flat", [P, BATCH, TT, D], F32)
        v_ring = sb("v_ring", [P, QUADS, TT, 4, 32], F32)
        q_ring = sb("q_ring", [P, QUADS, 2, 2, SEQ], BF16)
        k_ring = sb("k_ring", [P, QUADS, 2, SEQ], BF16)
        neg_max = sb("neg_max", [P, 2, 16], F32)
        shift = sb("shift", [16, P], F32)
        shift_rest = sb("shift_rest", [16, P], F32)
        shift_parts = sb("shift_parts", [16, 3, P], BF16)
        probs = sb("probs", [P, TT, 4, SEQ], F32)
        out_t = sb("out_t", [P, SEQ], F32)
        weight = sb("weight", [P, TT, 4], F32)
        attended = sb("attended", [P, TT, D], F32)
        residual = sb("residual", [P, TT, D], F32)
        qk_rows = nc.dram_tensor("qk_rows", (BATCH, 2, SLOTS, P, SEQ), BF16).ap()

        prep_x_loaded = sem("prep_x_loaded")
        prep_stats_ready = sem("prep_stats_ready")
        prep_moments_ready = sem("prep_moments_ready")
        prep_rstd_ready = sem("prep_rstd_ready")
        prep_xn_ready = sem("prep_xn_ready")
        v_filled = sem("v_filled")
        ring_cleared = sem("ring_cleared")
        rope_step = sem("rope_step")
        roped = sem("roped")
        first_part_ready = sem("first_part_ready")
        rest_ready = sem("rest_ready")
        second_part_ready = sem("second_part_ready")
        parts_ready = sem("parts_ready")
        parts_written = [sem(f"parts_written{c}") for c in range(2)]
        quad_loaded = [sem(f"quad_loaded{g}") for g in range(QUADS)]
        shift_loaded = sem("shift_loaded")
        max_placed = sem("max_placed")
        max_used = sem("max_used")
        shift_step = sem("shift_step")
        shift_ready = sem("shift_ready")
        ring_placed = sem("ring_placed")
        ring_used = sem("ring_used")
        o_placed = sem("o_placed")
        o_kept = sem("o_kept")
        o_turned = sem("o_turned")
        weight_ready = sem("weight_ready")
        attended_ready = sem("attended_ready")
        residual_loaded = sem("residual_loaded")
        x2_ready = sem("x2_ready")
        x2_passed = sem("x2_passed")

        block = ctx.enter_context(nc.Block())


        def pass_wait(eng):
            eng.sem_inc(waits_passed, 1)

        def measure(dve, steps, s):
            for t in range(TT):
                i = nc.vector.bn_stats(stats[:, t, :], stage[:, s, t, 0:D])
            steps.did(i)
            steps.settle()
            pass_wait(dve)
            for t in range(TT):
                i = nc.vector.bn_aggr(moments[:, s % 2, t, :], stats[:, t, :])
            steps.did(i)
            steps.settle()
            nc.vector.tensor_scalar(spread[:, s % 2, :], moments[:, s % 2, :, 1], EPS, None, ALU.add
                                    ).then_inc(moments_ready, 1)

        def invert_deviation(pool, r, s):
            pool.wait_ge(moments_ready, r + 1)
            nc.gpsimd.tensor_tensor(rstd[:, s % 2, :], spread[:, s % 2, :], minus_half[:, :], ALU.pow
                                    ).then_inc(rstd_ready, 1)

        def normalize(eng, unit, r, s):
            eng.wait_ge(rstd_ready, r + 1)
            pass_wait(eng)
            for t in range(TT):
                i = unit.tensor_scalar(xn[:, s % 2, t, :], stage[:, s, t, 0:D], moments[:, s % 2, t, 0:1],
                                            rstd[:, s % 2, t:t + 1], ALU.subtract, ALU.mult)
            i.then_inc(xn_ready, 1)

        def choose(dve, steps, r, bank):
            logits = psum[:, bank, 0:TT * EXPERTS].rearrange("p (t e) -> p t e", e=EXPERTS)
            dve.wait_ge(logits_ready, r + 1)
            steps.did(nc.vector.tensor_reduce(top[:, :], logits, AX.X, ALU.max))
            steps.settle()
            nc.vector.tensor_tensor(below[:, :, :], logits, top[:, :].unsqueeze(2).broadcast_to([P, TT, EXPERTS]),
                                    ALU.subtract).then_inc(below_ready, 1)
            dve.wait_ge(below_ready, r + 1)
            steps.did(nc.vector.tensor_scalar(tied[:, :, :], below[:, :, :], 0.0, -float(EXPERTS),
                                              ALU.is_ge, ALU.mult))
            steps.settle()
            steps.did(nc.vector.tensor_tensor(tied[:, :, :], tied[:, :, :],
                                              iota_e[:, :].unsqueeze(1).broadcast_to([P, TT, EXPERTS]), ALU.add))
            steps.settle()
            steps.did(nc.vector.tensor_reduce(first[:, :], tied[:, :, :], AX.X, ALU.min))
            steps.settle()
            nc.vector.tensor_tensor(onehot[:, :, :], iota_low[:, :].unsqueeze(1).broadcast_to([P, TT, EXPERTS]),
                                    first[:, :].unsqueeze(2).broadcast_to([P, TT, EXPERTS]),
                                    ALU.is_equal).then_inc(onehot_ready, 1)
            steps.did(nc.vector.tensor_scalar(base[:, :], first[:, :], float(EXPERTS), float(CAP),
                                              ALU.add, ALU.mult))

        def route(dve, steps, r, s, bank, b):
            earlier = psum[:, bank, 64:64 + TT * EXPERTS].rearrange("p (t e) -> p t e", e=EXPERTS)
            total = psum[:, bank, 128:128 + EXPERTS]
            dve.wait_ge(place_ready, r + 1)
            dve.wait_ge(onehot_ready, r + 1)
            steps.did(nc.vector.tensor_tensor(place[:, :, :], earlier,
                                              carry[:, :].unsqueeze(1).broadcast_to([P, TT, EXPERTS]), ALU.add))
            steps.settle()
            steps.did(nc.vector.tensor_tensor(place[:, :, :], place[:, :, :], onehot[:, :, :], ALU.mult))
            steps.did(nc.vector.tensor_tensor(carry[:, :], total, carry[:, :], ALU.add))
            steps.settle()
            steps.did(nc.vector.tensor_reduce(loc[:, :], place[:, :, :], AX.X, ALU.add))
            dve.wait_ge(gate_exp_ready, r + 1)
            steps.did(nc.vector.tensor_reduce(gate_sum[:, :], gate_exp[:, :, :], AX.X, ALU.add))
            steps.settle()
            steps.did(nc.vector.tensor_tensor(base[:, :], base[:, :], loc[:, :], ALU.add))
            steps.did(nc.vector.tensor_scalar(over[:, :], loc[:, :], float(CAP), float(NOWHERE), ALU.is_ge, ALU.mult))
            steps.did(nc.vector.tensor_scalar(half[:, :], loc[:, :], float(CAP), 0.5, ALU.is_lt, ALU.mult))
            steps.did(nc.vector.reciprocal(gate_sum[:, :], gate_sum[:, :]))
            steps.settle()
            nc.vector.tensor_tensor(dest[:, s, :], base[:, :], over[:, :], ALU.add)
            nc.vector.tensor_tensor(stage[:, s, :, D + 1], half[:, :], gate_sum[:, :], ALU.mult)
            nc.vector.tensor_copy(stage[:, s, :, D].bitcast(I32),
                                  numbers[:, bass.ds(b * TT, TT)]).then_inc(route_ready, 1)

        def turn_tokens(pe, r, s, bank):
            pe.wait_ge(xn_ready, r + 1)
            for t in range(TT):
                i = nc.tensor.transpose(psum[:, bank, t * P:(t + 1) * P], xn[:, s % 2, t, :], ident[:, :])
            i.then_inc(xn_t_placed, 1)

        def gate_logits(pe, r, s, bank):
            pe.wait_ge(xn_t_ready, r + 1)
            for t in range(TT):
                i = nc.tensor.matmul(psum[:, bank, t * EXPERTS:(t + 1) * EXPERTS], xn_t[:, s % 2, t * P:(t + 1) * P],
                                     wg_sb[:, :], start=True, stop=True)
            i.then_inc(logits_ready, 1)

        def count_places(pe, r, bank):
            pe.wait_ge(onehot_ready, r + 1)
            flat = onehot[:, :, :].rearrange("p t e -> p (t e)")
            nc.tensor.matmul(psum[:, bank, 64:64 + TT * EXPERTS], counters[:, 0, :], flat, start=True, stop=False,
                             skip_group_check=True)
            for t in range(TT - 1):
                nc.tensor.matmul(psum[:, bank, 64 + (t + 1) * EXPERTS:64 + TT * EXPERTS], counters[:, 1, :],
                                 onehot[:, t, :].unsqueeze(1).broadcast_to([P, TT - 1 - t, EXPERTS]),
                                 start=False, stop=t == TT - 2, skip_group_check=True)
            for t in range(TT):
                i = nc.tensor.matmul(psum[:, bank, 128:128 + EXPERTS], counters[:, 1, :], onehot[:, t, :],
                                     start=False, stop=t == TT - 1, skip_group_check=True)
            i.then_inc(place_ready, 1)

        def keep_turned(act, r, s, bank):
            act.wait_ge(xn_t_placed, r + 1)
            nc.scalar.copy(xn_t[:, s % 2, :], psum[:, bank, :]).then_inc(xn_t_ready, 1)

        def gate_exponentials(act, r):
            act.wait_ge(below_ready, r + 1)
            nc.scalar.activation(gate_exp[:, :, :], below[:, :, :], ACT.Exp).then_inc(gate_exp_ready, 1)

        def scatter_tokens(pool, r, s, layer):
            pool.wait_ge(route_ready, r + 1)
            pass_wait(pool)
            for t in range(TT):
                pool.indirect_dma_start(
                    out=slots[layer][:, :],
                    out_offset=bass.IndirectOffsetOnAxis(ap=dest[:, s, t:t + 1].bitcast(U32), axis=0),
                    in_=stage[:, s, t, :], in_offset=None, bounds_check=TOKENS - 1,
                    oob_is_err=False).then_inc(dispatched[s], 16)


        def load_w1(sp, layer, i, k):
            sp.wait_ge(w1_used, i * UNROLL + (layer * EXPERTS + k + 1))
            sp.dma_start(w1_ring[:, k, :], w1[i * UNROLL + k]).then_inc(w1_loaded[k], 16)

        def load_slots(sp, layer, i, k):
            sp.wait_ge(y_used, i * UNROLL + (layer * EXPERTS + k + 1))
            sp.dma_start(slot_rows[:, k, :, :],
                         slots[layer][bass.ds((i * UNROLL + k) * CAP, CAP), :].rearrange("(s p) c -> p s c", p=P)
                         ).then_inc(slots_loaded[k], 16)

        def load_experts(sp, layer):
            for s in range(STAGES):
                sp.wait_ge(dispatched[s], all_dispatched(s, layer))
            for k in range(UNROLL):
                load_slots(sp, layer, 0, k)
            with sp.Fori(0, EXPERTS // UNROLL - 1) as i:
                for k in range(UNROLL):
                    load_w1(sp, layer, i + 1, k)
                    load_slots(sp, layer, i + 1, k)

        def all_dispatched(s, layer):
            return 16 * TT * (BATCH // STAGES + BATCH * layer * (s == 0))

        def measure_slots(dve, n, turn, k):
            dve.wait_ge(slots_loaded[k], (turn + 1) * 16)
            for s in range(ST):
                i = nc.vector.bn_stats(slot_stats[:, s, :], slot_rows[:, k, s, 0:D])
            i.then_inc(slot_stats_ready, 1)
            dve.wait_ge(slot_stats_ready, 2 * n + 1)
            pass_wait(dve)
            for s in range(ST):
                i = nc.vector.bn_aggr(slot_moments[:, k % 2, s, :], slot_stats[:, s, :])
            i.then_inc(slot_stats_ready, 1)
            dve.wait_ge(slot_stats_ready, 2 * n + 2)
            nc.vector.tensor_scalar(slot_spread[:, k % 2, :], slot_moments[:, k % 2, :, 1], EPS, None, ALU.add
                                    ).then_inc(slot_moments_ready, 1)

        def invert_slot_deviation(pool, n, k):
            pool.wait_ge(slot_moments_ready, n + 1)
            nc.gpsimd.tensor_tensor(slot_rstd[:, k % 2, :], slot_spread[:, k % 2, :], minus_half[:, 0:ST], ALU.pow
                                    ).then_inc(slot_rstd_ready, 1)

        def normalize_slots(dve, n, k):
            dve.wait_ge(slot_rstd_ready, n + 1)
            for s in range(ST):
                i = nc.vector.tensor_scalar(slot_xn[:, k % 2, s, :], slot_rows[:, k, s, 0:D],
                                            slot_moments[:, k % 2, s, 0:1], slot_rstd[:, k % 2, s:s + 1],
                                            ALU.subtract, ALU.mult)
            i.then_inc(slot_xn_ready, 1)

        def add_expert(dve, n, turn, k):
            dve.wait_ge(y_placed, n + 1)
            dve.wait_ge(rows_written[k], turn * (16 * ST))
            nc.vector.tensor_copy(new_rows[:, k, :, D].bitcast(I32), slot_rows[:, k, :, D].bitcast(I32))
            for s in range(ST):
                i = nc.vector.scalar_tensor_tensor(new_rows[:, k, s, 0:D], psum[:, 6 + k % 2, s * D:(s + 1) * D],
                                                   slot_rows[:, k, s, D + 1:D + 2], slot_rows[:, k, s, 0:D],
                                                   ALU.mult, ALU.add)
            i.then_inc(y_used, 1)

        def turn_slots(pe, n, k):
            pe.wait_ge(slot_xn_ready, n + 1)
            for s in range(ST):
                i = nc.tensor.transpose(psum[:, k % 2, s * P:(s + 1) * P], slot_xn[:, k % 2, s, :], ident[:, :])
            i.then_inc(slot_xn_t_placed, 1)

        def expert_in(pe, n, turn, k):
            pe.wait_ge(slot_xn_t_ready, n + 1)
            pe.wait_ge(w1_loaded[k], (turn + 1) * 16)
            for c in range(FC):
                i = nc.tensor.matmul(psum[:, 2 + 2 * (k % 2) + c // 2, (c % 2) * CAP:(c % 2 + 1) * CAP],
                                     w1_ring[:, k, c * P:(c + 1) * P], slot_xn_t[:, k % 2, :],
                                     start=True, stop=True)
                if c % 2 == 1:
                    i.then_inc(hidden_placed, 1)

        def expert_out(pe, n, e, k, turn_next):
            pe.wait_ge(hidden_ready, 2 * n + 2)
            pe.wait_ge(y_used, n + (UNROLL - 1))
            for s in range(ST):
                for c in range(FC):
                    if turn_next and (s, c) == (ST - 1, FC - 2):
                        turn_slots(pe, n + 2, (k + 2) % UNROLL)
                    i = nc.tensor.matmul(psum[:, 6 + k % 2, s * D:(s + 1) * D], hidden[:, k % 2, c, s * P:(s + 1) * P],
                                         w2_sb[:, e, c, :], start=c == 0, stop=c == FC - 1)
                    if s == 0 and c == 0:
                        i.then_inc(w1_used, 1)
            i.then_inc(y_placed, 1)

        def keep_slots_turned(act, n, k):
            act.wait_ge(slot_xn_t_placed, n + 1)
            nc.scalar.copy(slot_xn_t[:, k % 2, :], psum[:, k % 2, 0:CAP]).then_inc(slot_xn_t_ready, 1)

        def rectify(act, n, k):
            for c in range(0, FC, 2):
                act.wait_ge(hidden_placed, 2 * n + c // 2 + 1)
                nc.scalar.activation(hidden[:, k % 2, c:c + 2, :],
                                     psum[:, 2 + 2 * (k % 2) + c // 2, :].rearrange("p (c n) -> p c n", c=2),
                                     ACT.Relu).then_inc(hidden_ready, 1)

        def scatter_rows(pool, n, k, layer):
            pool.wait_ge(y_used, n + (UNROLL + 1))
            pass_wait(pool)
            for s in range(ST):
                pool.indirect_dma_start(
                    out=rows_of[layer][:, :],
                    out_offset=bass.IndirectOffsetOnAxis(ap=new_rows[:, k, s, D:D + 1].bitcast(U32), axis=0),
                    in_=new_rows[:, k, s, 0:D], in_offset=None, bounds_check=TOKENS - 1,
                    oob_is_err=False).then_inc(rows_written[k], 16)

        def pool_experts(pool, layer):
            def body(i, last):
                for k in range(UNROLL):
                    n = i * UNROLL + (layer * EXPERTS + k)
                    if not (last and k + 3 >= UNROLL):
                        invert_slot_deviation(pool, n + 3, (k + 3) % UNROLL)
                    scatter_rows(pool, n, k, layer)
            n = layer * EXPERTS
            for k in range(3):
                invert_slot_deviation(pool, n + k, k)
            with pool.Fori(0, EXPERTS // UNROLL - 1) as i:
                body(i, False)
            body(EXPERTS // UNROLL - 1, True)

        def pe_experts(pe, layer):
            def body(i, last):
                for k in range(UNROLL):
                    e = i * UNROLL + k
                    n = i * UNROLL + (layer * EXPERTS + k)
                    turn = i + layer * (EXPERTS // UNROLL)
                    if not (last and k + 1 >= UNROLL):
                        expert_in(pe, n + 1, turn + (k + 1) // UNROLL, (k + 1) % UNROLL)
                    expert_out(pe, n, e, k, not (last and k + 2 >= UNROLL))
            n = layer * EXPERTS
            turn_slots(pe, n, 0)
            turn_slots(pe, n + 1, 1)
            expert_in(pe, n, layer * (EXPERTS // UNROLL), 0)
            with pe.Fori(0, EXPERTS // UNROLL - 1) as i:
                body(i, False)
            body(EXPERTS // UNROLL - 1, True)

        def act_experts(act, layer):
            def body(i, last):
                for k in range(UNROLL):
                    n = i * UNROLL + (layer * EXPERTS + k)
                    if not (last and k + 1 >= UNROLL):
                        rectify(act, n + 1, (k + 1) % UNROLL)
                    if not (last and k + 2 >= UNROLL):
                        keep_slots_turned(act, n + 2, (k + 2) % UNROLL)
            n = layer * EXPERTS
            keep_slots_turned(act, n, 0)
            keep_slots_turned(act, n + 1, 1)
            rectify(act, n, 0)
            with act.Fori(0, EXPERTS // UNROLL - 1) as i:
                body(i, False)
            body(EXPERTS // UNROLL - 1, True)

        def dve_experts(dve, layer):
            def body(i, last):
                for k in range(UNROLL):
                    n = i * UNROLL + (layer * EXPERTS + k)
                    turn = i + layer * (EXPERTS // UNROLL)
                    if not (last and k + 2 >= UNROLL):
                        measure_slots(dve, n + 2, turn + (k + 2) // UNROLL, (k + 2) % UNROLL)
                        dve.wait_ge(slot_xn_t_placed, n + 1)
                        normalize_slots(dve, n + 2, (k + 2) % UNROLL)
                    add_expert(dve, n, turn, k)
            n, turn = layer * EXPERTS, layer * (EXPERTS // UNROLL)
            for k in range(2):
                measure_slots(dve, n + k, turn, k)
            for k in range(2):
                normalize_slots(dve, n + k, k)
            with dve.Fori(0, EXPERTS // UNROLL - 1) as i:
                body(i, False)
            body(EXPERTS // UNROLL - 1, True)


        OUT_T, MISC, RING, MAXIMA = 0, 1, 2, 4

        class Place:

            def __init__(self, base, at):
                self.bank = RING + at % 2
                self.free = base + (at + 1)
                self.placed = base + (at + 1)
                self.kept = base + (at + 3)

        def batch_places(prep, follows):
            beside = {(g, 1): ("shift", g) for g in range(QUADS) if g < 3 or follows}
            if prep:
                beside |= {(1, 4): "turn", (1, 9): ("project", 0), (1, 12): ("project", 1), (2, 4): ("project", 2),
                           (2, 9): ("project", 3), (2, 12): "v"}
            order = []
            for g in range(QUADS):
                for u in range(16):
                    order.append((g, u))
                    if (g, u) in beside:
                        order.append(beside[g, u])
            return order

        PREPARED = ("turn", ("project", 0), ("project", 1), ("project", 2), ("project", 3), "v")
        FIRST_SHIFT = Place(2 * len(PREPARED), 0)
        WHOLE_BATCH = len(batch_places(True, True))
        assert WHOLE_BATCH % 2 == 0 and len(PREPARED) % 2 == 0

        def prologue_place(n, what):
            return Place(n * len(PREPARED), PREPARED.index(what))

        def ring_base(b):
            base = b * WHOLE_BATCH + 2 * len(PREPARED)
            return base - len(PREPARED) if isinstance(b, int) and b == BATCH - 1 else base

        def batch_place(b, prep, follows, what):
            return Place(ring_base(b), 1 + batch_places(prep, follows).index(what))

        def before_batch(b):
            return ring_base(b) + 1

        def load_prep(sp, n):
            sp.wait_ge(prep_xn_ready, n)
            sp.dma_start(prep_x[:, :, :], x1[bass.ds(n * SEQ, SEQ), :].rearrange("(t p) d -> p t d", p=P)
                         ).then_inc(prep_x_loaded, 16)

        def prep_measure(dve, n):
            dve.wait_ge(prep_x_loaded, (n + 1) * 16)
            for t in range(TT):
                i = nc.vector.bn_stats(prep_stats[:, t, :], prep_x[:, t, :])
            i.then_inc(prep_stats_ready, 1)
            dve.wait_ge(prep_stats_ready, n * 2 + 1)
            pass_wait(dve)
            for t in range(TT):
                i = nc.vector.bn_aggr(prep_moments[:, t, :], prep_stats[:, t, :])
            i.then_inc(prep_stats_ready, 1)
            dve.wait_ge(prep_stats_ready, n * 2 + 2)
            nc.vector.tensor_scalar(prep_spread[:, :], prep_moments[:, :, 1], EPS, None, ALU.add
                                    ).then_inc(prep_moments_ready, 1)

        def prep_invert(pool, n):
            pool.wait_ge(prep_moments_ready, n + 1)
            nc.gpsimd.tensor_tensor(prep_rstd[:, :], prep_spread[:, :], minus_half[:, :], ALU.pow
                                    ).then_inc(prep_rstd_ready, 1)

        def prep_normalize(eng, unit, n, turned_before):
            eng.wait_ge(prep_rstd_ready, n + 1)
            eng.wait_ge(ring_placed, turned_before)
            pass_wait(eng)
            for t in range(TT):
                i = unit.tensor_scalar(prep_xn[:, t, :], prep_x[:, t, :], prep_moments[:, t, 0:1],
                                       prep_rstd[:, t:t + 1], ALU.subtract, ALU.mult)
            i.then_inc(prep_xn_ready, 1)

        def prep_turn(pe, n, place):
            pe.wait_ge(prep_xn_ready, n + 1)
            pe.wait_ge(ring_used, place.free)
            for t in range(TT):
                i = nc.tensor.transpose(psum[:, place.bank, t * P:(t + 1) * P], prep_xn[:, t, :], ident[:, :])
            i.then_inc(ring_placed, 1)

        def prep_keep_turned(act, place):
            act.wait_ge(ring_placed, place.placed)
            nc.scalar.copy(prep_xn_t[:, :], psum[:, place.bank, :]).then_inc(ring_used, 1)

        def project(pe, c, turn, place):
            pe.wait_ge(ring_used, turn.kept)
            pe.wait_ge(ring_used, place.free)
            w = (wq_sb, wk_sb)[c // 2][:, c % 2, :]
            nc.tensor.matmul(psum[:, place.bank, :], w, prep_xn_t[:, :], start=True, stop=True).then_inc(ring_placed, 1)

        def keep_projection(act, n, c, place):
            act.wait_ge(ring_placed, place.placed)
            act.wait_ge(roped, n * 2 + (1 + c // 2))
            nc.scalar.activation(proj[:, c, :], psum[:, place.bank, :], ACT.Identity, bias=bias_sb[:, c:c + 1]
                                 ).then_inc(ring_used, 1)

        def project_v(pe, turn, place):
            pe.wait_ge(ring_used, turn.kept)
            pe.wait_ge(ring_used, place.free)
            for t in range(TT):
                i = nc.tensor.matmul(psum[:, place.bank, t * D:(t + 1) * D], prep_xn_t[:, t * P:(t + 1) * P],
                                     wv_sb[:, :], start=True, stop=True)
            i.then_inc(ring_placed, 1)

        def keep_v(act, n, place):
            act.wait_ge(ring_placed, place.placed)
            nc.scalar.copy(v_flat[:, bass.ds(n, 1), :, :].squeeze(1),
                           psum[:, place.bank, :].rearrange("p (t d) -> p t d", t=TT)).then_inc(ring_used, 1)

        def rotate(eng, unit, n, c, place):
            eng.wait_ge(ring_used, place.kept)
            unit.tensor_tensor(proj[:, 2 * c, :], proj[:, 2 * c, :], rope_sb[:, 0, :], ALU.mult)
            unit.tensor_tensor(proj[:, 2 * c + 1, :], proj[:, 2 * c + 1, :], rope_sb[:, 1, :], ALU.mult
                                    ).then_inc(rope_step, 1)
            eng.wait_ge(rope_step, n * 2 + (c + 1))
            unit.tensor_tensor(turned[:, c, :], proj[:, 2 * c, :], proj[:, 2 * c + 1, :], ALU.add
                                    ).then_inc(roped, 1)

        def keep_first_part(eng, unit, n, c):
            eng.wait_ge(roped, n * 2 + (c + 3))
            eng.wait_ge(parts_written[c], n * (16 * len(PART_SLOTS[c])))
            pass_wait(eng)
            unit.tensor_copy(parts[:, c, 0, :], turned[:, c, :]).then_inc(first_part_ready, 1)

        def take_rest(eng, unit, n, c):
            eng.wait_ge(first_part_ready, n * 2 + (c + 1))
            unit.tensor_tensor(turned[:, c, :], turned[:, c, :], parts[:, c, 0, :], ALU.subtract
                                    ).then_inc(rest_ready, 1)

        def keep_second_part(eng, unit, n, c):
            eng.wait_ge(rest_ready, n * 2 + (c + 1))
            pass_wait(eng)
            unit.tensor_copy(parts[:, c, 1, :], turned[:, c, :]).then_inc(second_part_ready, 1)

        def keep_third_part(eng, unit, n, c):
            eng.wait_ge(second_part_ready, n * 2 + (c + 1))
            unit.tensor_tensor(parts[:, c, 2, :], turned[:, c, :], parts[:, c, 1, :], ALU.subtract
                                    ).then_inc(parts_ready, 1)

        def split(eng, unit, n, c):
            keep_first_part(eng, unit, n, c)
            take_rest(eng, unit, n, c)
            keep_second_part(eng, unit, n, c)
            keep_third_part(eng, unit, n, c)

        def write_parts(sp, n, c):
            sp.wait_ge(parts_ready, n * 2 + (c + 1))
            for first, last, step, part in PART_SLOTS[c]:
                count = (last - first) // step + 1
                sp.dma_start(qk_rows[bass.ds(n, 1), c, first:last + 1:step, :, :].squeeze(0)
                             .rearrange("s f t -> f s t"),
                             parts[:, c, part, :].unsqueeze(1).broadcast_to([P, count, SEQ])
                             ).then_inc(parts_written[c], 16)

        def load_quad(sp, n, g):
            for c in range(2):
                sp.wait_ge(parts_written[c], (n + 1) * (16 * len(PART_SLOTS[c])))
                pass_wait(sp)
            for c in range(2):
                for h in range(2):
                    ring = (q_ring[:, g, h, :, :], k_ring[:, g, :, :])[c]
                    features = slice(16 * (2 * g + h), 16 * (2 * g + h + 1))
                    src = qk_rows[bass.ds(n, 1), c, :, features, :].squeeze(0)
                    sp.dma_start(ring[64 * h:64 * h + ROWS, :, :].rearrange("p h s -> p (h s)"),
                                 src.rearrange("s (d h) t -> s d (h t)", h=2)).then_inc(quad_loaded[g], 16)

        def fill_v(pool, n, g, kept):
            pool.wait_ge(ring_used, kept)
            flat = v_flat[:, bass.ds(n, 1), :, :].squeeze(1)
            nc.gpsimd.tensor_tensor(
                v_ring[:, g, :, :, 0:HEAD_DIM],
                flat[:, :, 32 * g:32 * g + 32].rearrange("p t (h d) -> p t h d", h=4),
                v_bias_sb[:, 32 * g:32 * g + 32].rearrange("p (h d) -> p h d", h=4).unsqueeze(1)
                .broadcast_to([P, TT, 4, HEAD_DIM]), ALU.add).then_inc(v_filled, 1)

        def max_tile(pe, q, g, w):
            h, tile = divmod(w // 2, TT)
            if w % 2 == 0:
                pe.wait_ge(max_used, q * 8 + (w // 2 + 1))
            i = nc.tensor.matmul(psum[:, MAXIMA + w % 4, :], q_ring[0:SHIFT_ROW, g, w % 2, h, tile * P:(tile + 1) * P],
                                 k_ring[0:SHIFT_ROW, g, h, :], start=True, stop=True)
            if w % 2 == 1:
                i.then_inc(max_placed, 1)

        def take_max(dve, q, g, pair):
            bank = MAXIMA + 2 * (pair % 2)
            dve.wait_ge(max_placed, q * 8 + (pair + 1))
            nc.vector.tensor_reduce(neg_max[:, g % 2, pair::TT * 2], psum[:, bank:bank + 2, :], AX.X, ALU.max,
                                    negate=True).then_inc(max_used, 1)

        def turn_shift(pe, q, g, place):
            pe.wait_ge(max_used, q * 8 + 10)
            pe.wait_ge(ring_used, place.free)
            nc.tensor.transpose(psum[0:16, place.bank, 0:P], neg_max[:, g % 2, :], ident[:, :]).then_inc(ring_placed, 1)

        def keep_shift(act, q, place):
            act.wait_ge(ring_placed, place.placed)
            act.wait_ge(shift_loaded, q * SHIFT_DMAS * 16)
            nc.scalar.copy(shift[:, :], psum[0:16, place.bank, 0:P])
            nc.scalar.copy(shift_parts[:, 0, :], psum[0:16, place.bank, 0:P]).then_inc(ring_used, 1)

        def split_shift(pool, q, place):
            pool.wait_ge(ring_used, place.kept)
            nc.gpsimd.tensor_tensor(shift_rest[:, :], shift[:, :], shift_parts[:, 0, :], ALU.subtract
                                    ).then_inc(shift_step, 1)
            pool.wait_ge(shift_step, q * 2 + 1)
            pass_wait(pool)
            nc.gpsimd.tensor_copy(shift_parts[:, 1, :], shift_rest[:, :]).then_inc(shift_step, 1)
            pool.wait_ge(shift_step, q * 2 + 2)
            nc.gpsimd.tensor_tensor(shift_parts[:, 2, :], shift_rest[:, :], shift_parts[:, 1, :], ALU.subtract
                                    ).then_inc(shift_ready, 1)

        def load_shift(sp, q, g):
            sp.wait_ge(shift_ready, q + 1)
            for part in range(3):
                row = SHIFT_ROW + part
                sp.dma_start(q_ring[row:row + 1, g, :, :, :].rearrange("p r h (t c) -> p (r h t) c", c=P),
                             shift_parts[:, part, :]).then_inc(shift_loaded, 16)

        def score_tile(pe, q, g, u, place):
            tile, head = divmod(u, 4)
            h = head // 2
            if u == 0:
                pe.wait_ge(shift_loaded, (q + 1) * SHIFT_DMAS * 16)
            pe.wait_ge(ring_used, place.free)
            nc.tensor.matmul(psum[:, place.bank, :], k_ring[:, g, h, tile * P:(tile + 1) * P],
                             q_ring[:, g, head % 2, h, :], start=True, stop=True).then_inc(ring_placed, 1)

        def exponential(act, u, place):
            act.wait_ge(ring_placed, place.placed)
            nc.scalar.activation(probs[:, u // 4, u % 4, :], psum[:, place.bank, :], ACT.Exp, scale=SCALE
                                 ).then_inc(ring_used, 1)

        def weigh(pe, q, g, tile):
            if tile == 0:
                pe.wait_ge(v_filled, q + 1)
                pe.wait_ge(o_kept, q)
            for head in range(4):
                i = nc.tensor.matmul(psum[32 * head:32 * head + 32, OUT_T, :], v_ring[:, g, tile, head, :],
                                     probs[:, tile, head, :], start=tile == 0, stop=tile == TT - 1,
                                     skip_group_check=True)
            if tile == TT - 1:
                i.then_inc(o_placed, 1)

        def keep_sums(act, q):
            act.wait_ge(o_placed, q + 1)
            nc.scalar.copy(out_t[:, :], psum[:, OUT_T, :]).then_inc(o_kept, 1)

        def turn_sums(pe, q):
            pe.wait_ge(o_kept, q + 1)
            for t in range(TT):
                i = nc.tensor.transpose(psum[:, MISC, t * P:(t + 1) * P], out_t[:, t * P:(t + 1) * P], ident[:, :])
            i.then_inc(o_turned, 1)

        def divide(dve, q, g):
            sums = psum[:, MISC, :].rearrange("p (t h c) -> p t h c", t=TT, h=4)
            dve.wait_ge(o_turned, q + 1)
            nc.vector.reciprocal(weight[:, :, :], sums[:, :, :, HEAD_DIM]).then_inc(weight_ready, 1)
            dve.wait_ge(weight_ready, q + 1)
            nc.vector.tensor_tensor(
                attended[:, :, 32 * g:32 * g + 32].rearrange("p t (h d) -> p t h d", h=4), sums[:, :, :, 0:HEAD_DIM],
                weight[:, :, :].unsqueeze(3).broadcast_to([P, TT, 4, HEAD_DIM]), ALU.mult).then_inc(attended_ready, 1)

        def load_residual(sp, b):
            sp.wait_ge(x2_ready, b)
            sp.dma_start(residual[:, :, :], x1[bass.ds(b * SEQ, SEQ), :].rearrange("(t p) d -> p t d", p=P)
                         ).then_inc(residual_loaded, 16)

        def add_residual(eng, unit, b):
            eng.wait_ge(residual_loaded, (b + 1) * 16)
            eng.wait_ge(attended_ready, b * 4 + 5)
            eng.wait_ge(dispatched[0], b * (16 * TT) + 16 * TT * (BATCH // STAGES))
            eng.wait_ge(x2_passed, b * 16 + 16)
            unit.tensor_tensor(stage[:, 0, :, 0:D], residual[:, :, :], attended[:, :, :], ALU.add
                               ).then_inc(x2_ready, 1)

        def pass_x2(sp, b):
            sp.wait_ge(x2_ready, b + 1)
            sp.dma_start(out[bass.ds(b * SEQ, SEQ), :].rearrange("(t p) d -> p t d", p=P), stage[:, 0, :, 0:D]
                         ).then_inc(x2_passed, 16)

        def pe_batch(pe, b, below, prep, follows):
            def place(*what):
                return batch_place(b, prep, follows, what if len(what) > 1 else what[0])
            for g in range(QUADS):
                q = b * 4 + g
                for u in range(16):
                    score_tile(pe, q, g, u, place(g, u))
                    if u % 4 in (1, 2) and (g < 2 or follows):
                        if u == 1:
                            pe.wait_ge(quad_loaded[(g + 2) % 4], (b + (1 + (g + 2) // 4)) * 64)
                        for w in range(2):
                            max_tile(pe, q + 2, (g + 2) % 4, u // 4 * 4 + (u % 4 - 1) * 2 + w)
                    if u == 1 and (g < 3 or follows):
                        turn_shift(pe, q + 1, (g + 1) % 4, place("shift", g))
                    if u % 4 == 3:
                        tile = (u // 4 + 3) % 4
                        if tile < 3:
                            weigh(pe, q, g, tile)
                        elif g > 0:
                            weigh(pe, q - 1, g - 1, tile)
                        elif below is not None:
                            weigh(pe, below * 4 + 3, 3, tile)
                    if u == 8:
                        if g == 2:
                            pe.wait_ge(below_ready, b + BATCH)
                        if g == 3:
                            pe.wait_ge(route_ready, b + BATCH)
                        if g > 0:
                            turn_sums(pe, q - 1)
                        elif below is not None:
                            turn_sums(pe, below * 4 + 3)
                    if prep:
                        if (g, u) == (1, 4):
                            prep_turn(pe, b + 2, place("turn"))
                        if (g, u) == (1, 9):
                            project(pe, 0, place("turn"), place("project", 0))
                        if (g, u) == (1, 12):
                            project(pe, 1, place("turn"), place("project", 1))
                        if (g, u) == (2, 4):
                            project(pe, 2, place("turn"), place("project", 2))
                        if (g, u) == (2, 9):
                            project(pe, 3, place("turn"), place("project", 3))
                        if (g, u) == (2, 12):
                            project_v(pe, place("turn"), place("v"))
                    if below is not None:
                        if (g, u) == (1, 13):
                            pe.wait_ge(attended_ready, q + 1)
                            turn_tokens(pe, below + BATCH, 0, MISC)
                        if (g, u) == (2, 0):
                            gate_logits(pe, below + BATCH, 0, MISC)
                        if (g, u) == (2, 13):
                            pe.wait_ge(attended_ready, q + 1)
                            count_places(pe, below + BATCH, MISC)

        def act_batch(act, b, below, prep, follows):
            def place(*what):
                return batch_place(b, prep, follows, what if len(what) > 1 else what[0])
            for g in range(QUADS):
                q = b * 4 + g
                for u in range(16):
                    exponential(act, u, place(g, u))
                    if u == 1 and (g < 3 or follows):
                        keep_shift(act, q + 1, place("shift", g))
                    if u == 3:
                        if g > 0:
                            keep_sums(act, q - 1)
                        elif below is not None:
                            keep_sums(act, below * 4 + 3)
                    if prep:
                        if (g, u) == (1, 4):
                            prep_keep_turned(act, place("turn"))
                        if (g, u) == (1, 9):
                            keep_projection(act, b + 2, 0, place("project", 0))
                        if (g, u) == (1, 12):
                            keep_projection(act, b + 2, 1, place("project", 1))
                        if (g, u) == (2, 4):
                            keep_projection(act, b + 2, 2, place("project", 2))
                        if (g, u) == (2, 9):
                            keep_projection(act, b + 2, 3, place("project", 3))
                        if (g, u) == (2, 12):
                            keep_v(act, b + 2, place("v"))
                    if below is not None:
                        if (g, u) == (1, 14):
                            keep_turned(act, below + BATCH, 0, MISC)
                        if (g, u) == (2, 3):
                            gate_exponentials(act, below + BATCH)

        def dve_batch(dve, b, below, prep, follows):
            r = None if below is None else below + BATCH
            for g in range(QUADS):
                q = b * 4 + g
                for pair in range(8):
                    if g < 2 or follows:
                        take_max(dve, q + 2, (g + 2) % 4, pair)
                    if (g, pair) == (0, 2) and prep:
                        prep_measure(dve, b + 2)
                    if pair == 4:
                        if g > 0:
                            divide(dve, q - 1, g - 1)
                        elif below is not None:
                            divide(dve, below * 4 + 3, 3)
                    if (g, pair) == (1, 1) and below is not None:
                        dve.wait_ge(x2_ready, b)
                        measure(dve, Steps(dve, route_step, route_start(r)), 0)
                    if (g, pair) == (2, 1) and below is not None:
                        choose(dve, Steps(dve, route_step, route_start(r) + 2), r, MISC)
                    if (g, pair) == (2, 7) and below is not None:
                        route(dve, Steps(dve, route_step, route_start(r) + 7), r, 0, MISC, below)

        def pool_batch(pool, b, below, prep, follows):
            r = None if below is None else below + BATCH
            v_kept = before_batch(b) + 2
            def place(*what):
                return batch_place(b, prep, follows, what)
            for g in range(QUADS):
                q = b * 4 + g
                if g < 3 or follows:
                    split_shift(pool, q + 1, place("shift", g))
                if g == 0 and below is not None:
                    pool.wait_ge(o_placed, q)
                    fill_v(pool, b, 3, v_kept)
                if g > 0 and follows:
                    pool.wait_ge(o_placed, q)
                    fill_v(pool, b + 1, g - 1, v_kept)
                if g == 0:
                    if prep:
                        prep_invert(pool, b + 2)
                        prep_normalize(pool, nc.gpsimd, b + 2, before_batch(b))
                    if below is not None:
                        add_residual(pool, nc.gpsimd, below)
                if g == 1 and below is not None:
                    invert_deviation(pool, r, 0)
                    pool.wait_ge(xn_t_placed, r)
                    normalize(pool, nc.gpsimd, r, 0)
                if g == 1 and prep:
                    rotate(pool, nc.gpsimd, b + 2, 0, place("project", 1))
                if g == 2 and prep:
                    split(pool, nc.gpsimd, b + 2, 0)
                    rotate(pool, nc.gpsimd, b + 2, 1, place("project", 3))
                if g == 3:
                    if prep:
                        split(pool, nc.gpsimd, b + 2, 1)
                    if below is not None:
                        scatter_tokens(pool, r, 0, 1)

        def sp_batch(sp, b, below, prep, follows):
            for g in range(QUADS):
                q = b * 4 + g
                if g == 0 and prep:
                    load_prep(sp, b + 2)
                if g == 0 or follows:
                    sp.wait_ge(ring_placed, before_batch(b) if g == 0 else
                               batch_place(b, prep, follows, (g - 1, 15)).placed)
                    pass_wait(sp)
                    load_quad(sp, b + (g > 0), (g + 3) % 4)
                if g < 3 or follows:
                    load_shift(sp, q + 1, (g + 1) % 4)
                if g == 0 and below is not None:
                    pass_x2(sp, below)
                    if follows:
                        for c in range(2):
                            write_parts(sp, b + 1, c)
                if g == 1:
                    load_residual(sp, b)

        def route_all(eng, body):
            with eng.Fori(0, BATCH // STAGES - 1) as i:
                for s in range(STAGES):
                    body(i * STAGES + s, i, s, False)
            for s in range(STAGES):
                body(BATCH - STAGES + s, BATCH // STAGES - 1, s, True)

        def route_start(r):
            return r * ROUTE_STEPS + 2

        def attend_all(eng, body):
            body(eng, 0, None, True, True)
            with eng.Fori(0, BATCH - 3) as below:
                body(eng, below + 1, below, True, True)
            body(eng, BATCH - 2, BATCH - 3, False, True)
            body(eng, BATCH - 1, BATCH - 2, False, False)

        LAST_QUAD = BATCH * QUADS - 1
        LAST_ROUTED = 2 * BATCH - 1

        routing_constants = [(ident[:, :], identity), (counters[:, :, :], count_mats), (iota_e[:, :], expert_iota[0]),
                             (iota_low[:, :], expert_iota[1]), (numbers[:, :], token_number), (wg_sb[:, :], wg)]
        attention_constants = [(wq_sb[:, :, :], wq_t), (wk_sb[:, :, :], wk_t), (wv_sb[:, :], wv_t),
                               (bias_sb[:, :], qk_bias), (v_bias_sb[:, :], v_bias.broadcast_to([P, D])),
                               (rope_sb[:, :, :], rope)]

        def load_x(sp, b, s):
            sp.dma_start(stage[:, s, :, 0:D], x[bass.ds(b * SEQ, SEQ), :].rearrange("(t p) d -> p t d", p=P)
                         ).then_inc(x_loaded[s], 16)

        def load_w2(eng, half):
            for e in range(half * EXPERTS // 2, (half + 1) * EXPERTS // 2, 4):
                eng.dma_start(w2_sb[:, e:e + 4, :, :], w2[e:e + 4].rearrange("e (c p) d -> p e c d", p=P)
                              ).then_inc(w2_loaded, 16)

        def clear_slots(eng, layer):
            eng.dma_start(slots[layer].rearrange("(n p) c -> p n c", p=P),
                          empty[:, :].unsqueeze(1).broadcast_to([P, TOKENS // P, ROW])
                          ).then_inc(slots_cleared[layer], 16)

        @block.sync
        def _(sp):
            for s in range(STAGES):
                load_x(sp, s, s)
            for dst, src in attention_constants:
                sp.dma_start(dst, src).then_inc(weights_loaded, 16)
            for k in range(UNROLL):
                load_w1(sp, 0, 0, k)
            with sp.Fori(0, BATCH // STAGES - 1) as i:
                for s in range(STAGES):
                    sp.wait_ge(dispatched[s], i * (16 * TT) + 16 * TT)
                    load_x(sp, i * STAGES + (STAGES + s), s)
            load_experts(sp, 0)
            for k in range(UNROLL):
                load_w1(sp, 1, 0, k)
            for k in range(UNROLL):
                sp.wait_ge(rows_written[k], 16 * ST * (EXPERTS // UNROLL))
            sp.wait_ge(ring_cleared, 3)
            load_prep(sp, 0)
            load_prep(sp, 1)
            for c in range(2):
                write_parts(sp, 0, c)
            for g in range(3):
                load_quad(sp, 0, g)
            for c in range(2):
                write_parts(sp, 1, c)
            load_shift(sp, 0, 0)
            attend_all(sp, sp_batch)
            pass_x2(sp, BATCH - 1)
            load_experts(sp, 1)
            for k in range(UNROLL):
                sp.wait_ge(rows_written[k], 2 * 16 * ST * (EXPERTS // UNROLL))

        @block.gpsimd
        def _(pool):
            nc.gpsimd.memset(minus_half[:, :], -0.5).then_inc(empty_ready, 1)
            nc.gpsimd.memset(empty[:, :], 0.0).then_inc(empty_ready, 1)
            pool.wait_ge(empty_ready, 2)
            nc.gpsimd.memset(empty[:, D:D + 1].bitcast(I32), NOWHERE).then_inc(empty_ready, 1)

            def body(b, i, s, last):
                if s + 2 < STAGES or not last:
                    invert_deviation(pool, b + 2, s)
                scatter_tokens(pool, b, s, 0)
            for s in range(2):
                invert_deviation(pool, s, s)
            pool.wait_ge(slots_cleared[0], 16)
            route_all(pool, body)
            nc.gpsimd.memset(q_ring[:, :, :, :, :], 0.0).then_inc(ring_cleared, 1)
            pool.wait_ge(x_passed, 16)
            pool_experts(pool, 0)
            pool.wait_ge(slots_cleared[1], 16)
            pool.wait_ge(weights_loaded, 16 * len(attention_constants))
            for n in range(2):
                prep_invert(pool, n)
            for g in range(QUADS):
                fill_v(pool, 0, g, prologue_place(0, "v").kept)
            pool.wait_ge(parts_ready, 2)
            for c in range(2):
                rotate(pool, nc.gpsimd, 1, c, prologue_place(1, ("project", 2 * c + 1)))
                split(pool, nc.gpsimd, 1, c)
            split_shift(pool, 0, FIRST_SHIFT)
            attend_all(pool, pool_batch)
            invert_deviation(pool, LAST_ROUTED, 0)
            scatter_tokens(pool, LAST_ROUTED, 0, 1)
            pool.wait_ge(x2_passed, 16 + 16 * BATCH)
            pool_experts(pool, 1)

        @block.vector
        def _(dve):
            nc.vector.memset(carry[:, :], 0.0).then_inc(route_step, 1)
            dve.wait_ge(consts_loaded, 16 * len(routing_constants))

            def measure_staged(steps, i, s):
                dve.wait_ge(x_loaded[s], (i + 1) * 16)
                measure(dve, steps, s)

            def body(b, i, s, last):
                steps = Steps(dve, route_step, b * ROUTE_STEPS + (3 if last and s + 1 == STAGES else 5))
                if s + 2 < STAGES or not last:
                    measure_staged(steps, i + (s + 2) // STAGES, (s + 2) % STAGES)
                choose(dve, steps, b, 2 + s % 2)
                if s + 1 < STAGES or not last:
                    normalize(dve, nc.vector, b + 1, (s + 1) % STAGES)
                route(dve, steps, b, s, 2 + s % 2, b)
                assert last or steps.n == ROUTE_STEPS
            steps = Steps(dve, route_step, 1)
            for s in range(2):
                measure_staged(steps, 0, s)
            normalize(dve, nc.vector, 0, 0)
            route_all(dve, body)
            nc.vector.memset(carry[:, :], 0.0).then_inc(route_step, 1)
            nc.vector.memset(k_ring[:, :, :, :], 1.0).then_inc(ring_cleared, 1)
            nc.vector.memset(v_ring[:, :, :, :, HEAD_DIM:HEAD_DIM + 1], 1.0)
            nc.vector.memset(v_ring[:, :, :, :, HEAD_DIM + 1:], 0.0).then_inc(ring_cleared, 1)
            dve_experts(dve, 0)
            for n in range(2):
                prep_measure(dve, n)
                prep_normalize(dve, nc.vector, n, n)
            for c in range(2):
                rotate(dve, nc.vector, 0, c, prologue_place(0, ("project", 2 * c + 1)))
                split(dve, nc.vector, 0, c)
            for g in range(2):
                for pair in range(8):
                    take_max(dve, g, g, pair)
            attend_all(dve, dve_batch)
            divide(dve, LAST_QUAD, QUADS - 1)
            add_residual(dve, nc.vector, BATCH - 1)
            dve.wait_ge(x2_ready, BATCH)
            steps = Steps(dve, route_step, route_start(LAST_ROUTED))
            measure(dve, steps, 0)
            normalize(dve, nc.vector, LAST_ROUTED, 0)
            choose(dve, steps, LAST_ROUTED, MISC)
            route(dve, steps, LAST_ROUTED, 0, MISC, BATCH - 1)
            dve_experts(dve, 1)

        @block.scalar
        def _(act):
            for dst, src in routing_constants:
                act.dma_start(dst, src).then_inc(consts_loaded, 16)
            act.wait_ge(empty_ready, 3)
            clear_slots(act, 0)
            act.sem_inc(y_used, UNROLL)
            act.sem_inc(w1_used, UNROLL)
            act.sem_inc(roped, 2)
            act.sem_inc(max_used, 2)
            act.sem_inc(ring_used, 2)
            act.sem_inc(attended_ready, 1)
            act.sem_inc(x2_passed, 16)
            def body(b, i, s, last):
                gate_exponentials(act, b)
                if last and s == STAGES // 2:
                    act.dma_start(x1, x).then_inc(x_passed, 16)
                    load_w2(act, 1)
                if s + 1 < STAGES or not last:
                    keep_turned(act, b + 1, s + 1, (s + 1) % 2)
            keep_turned(act, 0, 0, 0)
            act.wait_ge(slots_cleared[0], 16)
            load_w2(act, 0)
            route_all(act, body)
            clear_slots(act, 1)
            act_experts(act, 0)
            act.wait_ge(weights_loaded, 16 * len(attention_constants))
            for n in range(2):
                prep_keep_turned(act, prologue_place(n, "turn"))
                for c in range(4):
                    keep_projection(act, n, c, prologue_place(n, ("project", c)))
                keep_v(act, n, prologue_place(n, "v"))
            keep_shift(act, 0, FIRST_SHIFT)
            attend_all(act, act_batch)
            keep_sums(act, LAST_QUAD)
            keep_turned(act, LAST_ROUTED, 0, MISC)
            gate_exponentials(act, LAST_ROUTED)
            act_experts(act, 1)

        @block.tensor
        def _(pe):
            pe.wait_ge(consts_loaded, 16 * len(routing_constants))

            def body(b, i, s, last):
                gate_logits(pe, b, s, 2 + s % 2)
                count_places(pe, b, 2 + s % 2)
                if s + 1 < STAGES or not last:
                    turn_tokens(pe, b + 1, s + 1, (s + 1) % 2)
            turn_tokens(pe, 0, 0, 0)
            route_all(pe, body)
            pe.wait_ge(w2_loaded, 16 * 4)
            pe_experts(pe, 0)
            pe.wait_ge(weights_loaded, 16 * len(attention_constants))
            with pe.Fori(0, 2) as n:
                turn = prologue_place(n, "turn")
                prep_turn(pe, n, turn)
                for c in range(4):
                    project(pe, c, turn, prologue_place(n, ("project", c)))
                project_v(pe, turn, prologue_place(n, "v"))
            pe.wait_ge(ring_cleared, 3)
            for g in range(2):
                pe.wait_ge(quad_loaded[g], 64)
                for w in range(16):
                    max_tile(pe, g, g, w)
                    if (g, w) == (1, 3):
                        turn_shift(pe, 0, 0, FIRST_SHIFT)
            attend_all(pe, pe_batch)
            pe.wait_ge(ring_used, batch_place(BATCH - 1, False, False, (QUADS - 1, 15)).kept)
            weigh(pe, LAST_QUAD, QUADS - 1, TT - 1)
            pe.wait_ge(attended_ready, LAST_QUAD + 1)
            turn_sums(pe, LAST_QUAD)
            pe.wait_ge(attended_ready, LAST_QUAD + 2)
            turn_tokens(pe, LAST_ROUTED, 0, MISC)
            gate_logits(pe, LAST_ROUTED, 0, MISC)
            count_places(pe, LAST_ROUTED, MISC)
            pe_experts(pe, 1)


def kernel(L0_attn_x, L0_attn_wq_w, L0_attn_wq_b, L0_attn_wk_w, L0_attn_wk_b, L0_attn_wv_w, L0_attn_wv_b,
           L0_ffn_Wg, L0_ffn_w1, L0_ffn_w2):
    import ml_dtypes
    import numpy as np
    import concourse.bacc as bacc
    from concourse.bass_utils import run_bass_kernel_spmd

    quad, par, feat, pair = np.meshgrid(np.arange(QUADS), np.arange(2), np.arange(HEAD_DIM), np.arange(2),
                                        indexing="ij")
    order = ((4 * quad + 2 * pair + par) * HEAD_DIM + feat).reshape(-1)
    partner = order ^ 1
    feature = feat.reshape(-1)

    theta = np.float32(10000.0) ** (np.float32(-2.0) * np.arange(HEAD_DIM // 2, dtype=np.float32)
                                    / np.float32(HEAD_DIM))
    angle = np.outer(np.arange(SEQ, dtype=np.float32), theta.astype(np.float32)).astype(np.float32)
    cosine = np.cos(angle).T[feature // 2]
    sine = np.sin(angle).T[feature // 2] * np.where(feature % 2 == 0, -1.0, 1.0)[:, None]

    a = np.asarray
    arrays = {
        "x": a(L0_attn_x).reshape(TOKENS, D),
        "wq_t": np.stack([a(L0_attn_wq_w)[order].T, a(L0_attn_wq_w)[partner].T], axis=1),
        "wk_t": np.stack([a(L0_attn_wk_w)[order].T, a(L0_attn_wk_w)[partner].T], axis=1),
        "wv_t": a(L0_attn_wv_w).T,
        "qk_bias": np.stack([a(L0_attn_wq_b)[order], a(L0_attn_wq_b)[partner],
                             a(L0_attn_wk_b)[order], a(L0_attn_wk_b)[partner]], axis=1),
        "v_bias": a(L0_attn_wv_b).reshape(1, D),
        "wg": a(L0_ffn_Wg),
        "w1": a(L0_ffn_w1),
        "w2": a(L0_ffn_w2),
        "rope": np.stack([cosine, sine], axis=1).astype(np.float32),
        "identity": np.eye(P, dtype=np.float32),
        "count_mats": np.stack([np.triu(np.ones((P, P)), 1), np.ones((P, P))], axis=1).astype(ml_dtypes.bfloat16),
        "expert_iota": np.stack([np.tile(np.arange(EXPERTS), (P, 1)), np.tile(np.arange(EXPERTS) - EXPERTS, (P, 1))]
                                ).astype(np.float32),
        "token_number": np.arange(TOKENS, dtype=np.int32).reshape(-1, P).T,
    }
    arrays = {name: np.ascontiguousarray(v) for name, v in arrays.items()}
    nc = bacc.Bacc("TRN2", target_bir_lowering=False, num_devices=1)
    args = [nc.dram_tensor(name, v.shape, mybir.dt.from_np(v.dtype), kind="ExternalInput").ap()
            for name, v in arrays.items()]
    out = nc.dram_tensor("out", (TOKENS, D), F32, kind="ExternalOutput").ap()
    macaron_block_kernel(nc, *args, out)
    r = run_bass_kernel_spmd(nc, [arrays], core_ids=[0])
    return r.results[0]["out"].reshape(BATCH, SEQ, D)
```
